# Optimizing a Trainium2 kernel written in Bass

```python
import numpy as np
import jax
import jax.numpy as jnp

def _softmax(x, axis=-1):
    return jax.nn.softmax(x, axis=axis)

def _gelu(x):
    return jax.nn.gelu(x, approximate=True)

def _silu(x):
    return jax.nn.silu(x)

def _sigmoid(x):
    return jax.nn.sigmoid(x)

def _layernorm(x, axis=-1, eps=1e-05):
    m = jnp.mean(x, axis=axis, keepdims=True)
    v = jnp.var(x, axis=axis, keepdims=True)
    return (x - m) / jnp.sqrt(v + eps)

def _scatter_add(tgt, idx, src, axis=0):
    return tgt.at[idx].add(src)

def _segment_sum(src, seg, n):
    return jax.ops.segment_sum(src, seg, n)
kernel_name = 'mk_xattn_ffn_d1_seqx_r2_4556ac'

def setup_inputs(seed: int=0):
    np.random.seed(seed)
    _w = jnp.asarray

    def _rec_inputs():
        import jax
        import jax.numpy as jnp
        _rk = jax.random.key(seed)
        x = -7.109e-05 + 0.9999 * jax.random.normal(jax.random.fold_in(_rk, 1), (4, 1024, 1024), jnp.float32)
        _lenS = 1024 - jax.random.randint(jax.random.fold_in(_rk, 7), (4,), 0, max(1, 1024 // 4) + 1, jnp.int32)
        _lenS2 = 1024 - jax.random.randint(jax.random.fold_in(_rk, 8), (4,), 0, max(1, 1024 // 4) + 1, jnp.int32)
        _ctx_512P = jax.random.normal(jax.random.fold_in(_rk, 11), (4, 16, 256), jnp.float32)
        _ctx_512c = jax.random.dirichlet(jax.random.fold_in(_rk, 511), 0.3 * jnp.ones((16,), jnp.float32), (4, 1024))
        _ctx_512t = jnp.einsum('bsk,bkd->bsd', _ctx_512c, _ctx_512P)
        _ctx_512t = _ctx_512t * jax.lax.rsqrt(jnp.mean(jnp.square(_ctx_512t)) + 1e-12) * 0.953939
        ctx_512 = 2.81802e-05 + 1.00001 * (_ctx_512t + 0.3 * jax.random.normal(jax.random.fold_in(_rk, 611), (4, 1024, 256), jnp.float32))
        return (x, ctx_512)
    x, ctx_512 = _rec_inputs()

    def _L0_xattn_setup():
        import jax, jax.numpy as jnp
        import numpy as np
        EPS = 1e-06
        IMAGE_DIMS = 1024
        key = jax.random.key(seed)
        k1, k2, k3 = jax.random.split(key, 3)
        B, I, J, D = (16, 1024, 1024, 256)
        p = jax.random.normal(k1, (B, I, J), dtype=jnp.float32)
        k_v = jax.random.normal(k2, (B, J, D), dtype=jnp.float32)
        W_k = jax.random.normal(k3, (D, D), dtype=jnp.float32) * (1.0 / np.sqrt(D))
        b_k = jnp.zeros((D,), dtype=jnp.float32)
        ln_gamma = jnp.ones((J,), dtype=jnp.float32)
        ln_beta = jnp.zeros((J,), dtype=jnp.float32)
        return {'p': p, 'k_v': k_v, 'W_k': W_k, 'b_k': b_k, 'ln_gamma': ln_gamma, 'ln_beta': ln_beta}
    _L0_xattn_all = _L0_xattn_setup()
    _L0_xattn_in = {k: v for k, v in _L0_xattn_all.items() if k in ('W_k', 'b_k', 'ln_gamma', 'ln_beta')}
    del _L0_xattn_all

    def _L0_ffn_setup():
        import jax, jax.numpy as jnp
        import numpy as np
        E = 8
        TOP_K = 2
        D = 1024
        M = 3584
        B, S = (2, 1024)
        key = jax.random.key(seed)
        kx, kg, k1, k2, k3 = jax.random.split(key, 5)
        x = jax.random.normal(kx, (B, S, D), dtype=jnp.float32)
        gate_w = jax.random.normal(kg, (D, E), dtype=jnp.float32) / np.sqrt(D)
        w1 = jax.random.normal(k1, (E, D, M), dtype=jnp.float32) / np.sqrt(D)
        w2 = jax.random.normal(k2, (E, M, D), dtype=jnp.float32) / np.sqrt(M)
        w3 = jax.random.normal(k3, (E, D, M), dtype=jnp.float32) / np.sqrt(D)
        return {'x': x, 'gate_w': gate_w, 'w1': w1, 'w2': w2, 'w3': w3}
    _L0_ffn_all = _L0_ffn_setup()
    _L0_ffn_in = {k: v for k, v in _L0_ffn_all.items() if k in ('gate_w', 'w1', 'w2', 'w3')}
    del _L0_ffn_all
    return {'x': x, 'ctx_512': ctx_512, 'L0_xattn_W_k': _L0_xattn_in['W_k'], 'L0_xattn_b_k': _L0_xattn_in['b_k'], 'L0_xattn_ln_gamma': _L0_xattn_in['ln_gamma'], 'L0_xattn_ln_beta': _L0_xattn_in['ln_beta'], 'L0_ffn_gate_w': _L0_ffn_in['gate_w'], 'L0_ffn_w1': _L0_ffn_in['w1'], 'L0_ffn_w2': _L0_ffn_in['w2'], 'L0_ffn_w3': _L0_ffn_in['w3']}

def reference(x, ctx_512, L0_xattn_W_k, L0_xattn_b_k, L0_xattn_ln_gamma, L0_xattn_ln_beta, L0_ffn_gate_w, L0_ffn_w1, L0_ffn_w2, L0_ffn_w3):
    import jax
    import jax.numpy as jnp

    def _L0_xattn_ref(p, k_v, W_k, b_k, ln_gamma, ln_beta):
        import jax, jax.numpy as jnp
        import numpy as np
        EPS = 1e-06
        IMAGE_DIMS = 1024
        kv = k_v @ W_k.T + b_k
        out = jnp.einsum('bij,bjd->bid', p, kv)
        scale = IMAGE_DIMS ** (-0.5)
        sim = jnp.einsum('bid,bjd->bij', out, kv) * scale
        mu = jnp.mean(sim, axis=-1, keepdims=True)
        var = jnp.var(sim, axis=-1, keepdims=True)
        sim = (sim - mu) * jax.lax.rsqrt(var + EPS) * ln_gamma + ln_beta
        attn = jax.nn.softmax(sim, axis=-1)
        return attn

    def _L0_ffn_ref(x, gate_w, w1, w2, w3):
        import jax, jax.numpy as jnp
        import numpy as np
        E = 8
        TOP_K = 2
        D = 1024
        M = 3584
        B, S = (2, 1024)
        b, s, d = x.shape
        x_flat = x.reshape(-1, d)
        router_logits = x_flat @ gate_w
        router_probs = jax.nn.softmax(router_logits, axis=-1)
        topk_w, topk_idx = jax.lax.top_k(router_probs, TOP_K)
        topk_w = topk_w / jnp.sum(topk_w, axis=-1, keepdims=True)
        idx_flat = topk_idx.reshape(-1)
        sort_idx = jnp.argsort(idx_flat)
        x_rep_sort = jnp.take(x_flat, sort_idx // TOP_K, axis=0)
        group_sizes = jnp.bincount(idx_flat, length=E).astype(jnp.int32)
        h = jax.lax.ragged_dot(x_rep_sort, w1, group_sizes)
        h = jax.nn.silu(h) * jax.lax.ragged_dot(x_rep_sort, w3, group_sizes)
        out_sort = jax.lax.ragged_dot(h, w2, group_sizes)
        inv_sort_idx = jnp.argsort(sort_idx)
        out_rep = jnp.take(out_sort, inv_sort_idx, axis=0).reshape(-1, TOP_K, d)
        out = jnp.einsum('tkd,tk->td', out_rep, topk_w)
        return out.reshape(b, s, d)
    x = x + _L0_xattn_ref(_layernorm(x, axis=-1), ctx_512, L0_xattn_W_k, L0_xattn_b_k, L0_xattn_ln_gamma, L0_xattn_ln_beta)
    x = x + _L0_ffn_ref(_layernorm(x, axis=-1), L0_ffn_gate_w, L0_ffn_w1, L0_ffn_w2, L0_ffn_w3)
    return x

_drawn_inputs = setup_inputs


def setup_inputs(seed=0):
    import zlib

    import numpy as np

    out = dict(_drawn_inputs(seed))
    spreads = {'L0_xattn_b_k': (0.0, 2.0),
     'L0_xattn_ln_gamma': (1.0, 0.6),
     'L0_xattn_ln_beta': (0.0, 2.0)}
    factors = {'ctx_512': 4.745, 'L0_xattn_W_k': 8.0}
    for name, (base, spread) in spreads.items():
        noise = np.random.default_rng([zlib.crc32(name.encode()), seed]).standard_normal(out[name].shape)
        drawn = base * np.exp(spread * noise) if base else spread * noise
        out[name] = jnp.asarray(drawn.astype(out[name].dtype))
    for name, factor in factors.items():
        out[name] = (out[name] * factor).astype(out[name].dtype)
    return out
```

```python
import concourse.bass as bass
from concourse import mybir
from contextlib import ExitStack

F32 = mybir.dt.float32
F32R = mybir.dt.float32r
I32 = mybir.dt.int32
U32 = mybir.dt.uint32
ALU = mybir.AluOpType
ACT = mybir.ActivationFunctionType
AX = mybir.AxisListType

P = 128
BATCH, SEQ, D = 4, 1024, 1024
CD = 256
E, M = 8, 3584
T = BATCH * SEQ
KT = D // P
MT = M // P
BANK = 512
UNIT = 4
UNITS = SEQ // (UNIT * P)
BT = SEQ // P
LIST = T
NOROW = T
SB = 3
PADROW = E * LIST
TAB = E * LIST + 4 * P
SLOTS = (2 * T // P + E + 2 * E) // SB
META = 32
assert SLOTS < META
LN_EPS, SIM_EPS = 1e-5, 1e-6
SIM_SCALE = 1024 ** -0.5


class Chain:

    def __init__(self, eng, sem, base, per_pass):
        self.eng, self.sem, self.base, self.n, self.per_pass = eng, sem, base, 0, per_pass

    def __call__(self, ins):
        self.n += 1
        ins.then_inc(self.sem, 1)
        self.eng.wait_ge(self.sem, self.base + self.n)

    def close(self):
        assert self.n == self.per_pass, (self.n, self.per_pass)


def attend_and_route(nc, x, ctx_in, W_k, b_k, gamma, beta, gate_w, x1_out, x2_rows, table, meta):
    RING_PRE = 2
    RING_B = 12 + UNITS * 18

    with ExitStack() as st:
        def sb(name, shape, dt=F32):
            return st.enter_context(nc.sbuf_tensor(name, shape, dt))

        def sem(name):
            return st.enter_context(nc.semaphore(name))

        xin = sb("xin", [P, UNITS, UNIT, D])
        ctxt = sb("ctxt", [P, BT, CD])
        wk_in = sb("wk_in", [P, 2, CD])
        wkT = sb("wkT", [P, 2, CD])
        bk_row = sb("bk_row", [1, CD])
        ones_row = sb("ones_row", [1, BANK])
        gam = sb("gam", [P, D])
        bet = sb("bet", [P, D])
        gw = sb("gw", [P, KT, E])
        ident = sb("ident", [P, P])
        onesm = sb("onesm", [P, P])
        before = sb("before", [P, P])
        ctxT = sb("ctxT", [P, 2, SEQ])
        kvT = sb("kvT", [P, 2, SEQ])
        kv = sb("kv", [P, BT, CD])
        pn = sb("pn", [P, 2, D])
        pT = sb("pT", [P, KT, UNIT * P])
        oT = sb("oT", [P, 2, UNIT * P])
        z = sb("z", [P, 2, D])
        x1 = sb("x1", [P, 2, D])
        x2 = sb("x2", [P, 2, D])
        x2T = sb("x2T", [P, 2, KT, P])
        st_a = sb("st_a", [P, UNIT, 2, 6])
        mv_a = sb("mv_a", [P, UNIT, 2])
        rs_a = sb("rs_a", [P, UNIT])
        st_s = sb("st_s", [P, 2, 2, 6])
        mv_s = sb("mv_s", [P, 2, 2])
        rs_s = sb("rs_s", [P, 2])
        st_b = sb("st_b", [P, 2, 2, 6])
        mv_b = sb("mv_b", [P, 2, 2])
        rs_b = sb("rs_b", [P, 2])
        ve = sb("ve", [P, 12])
        mhalf = sb("mhalf", [P, UNIT])
        leps = sb("leps", [P, UNIT])
        seps = sb("seps", [P, 1])
        nmx = sb("nmx", [P, 2])
        esum = sb("esum", [P, 2])
        rsum = sb("rsum", [P, 2])
        lg = sb("lg", [P, BT, E])
        pr = sb("pr", [P, BT, E])
        t0 = sb("t0", [P, BT, E])
        oh1 = sb("oh1", [P, BT, E])
        oh2 = sb("oh2", [P, BT, E])
        both = sb("both", [P, BT, E])
        m1 = sb("m1", [P, BT])
        m2 = sb("m2", [P, BT])
        mk = sb("mk", [P, BT])
        msum = sb("msum", [P, BT])
        posf = sb("posf", [P, 2, BT])
        posi = sb("posi", [P, 2, BT], I32)
        rec = sb("rec", [P, 2, BT, 2], I32)
        rowid = sb("rowid", [P, BT], I32)
        seqs = sb("seqs", [P, BT], I32)
        pref = sb("pref", [P, E], I32)
        preff = sb("preff", [P, E])
        eidf = sb("eidf", [P, E])
        ebase = sb("ebase", [P, E])
        lbase = sb("lbase", [P, E])
        empty = sb("empty", [P, TAB // P, 2], I32)
        zrow = sb("zrow", [1, D])
        c8 = sb("c8", [P, 12, E])
        i8 = sb("i8", [P, 2, E], I32)
        sidx = sb("sidx", [1, META, E], I32)
        sl = sb("sl", [1, 8, META, E])
        metaf = sb("metaf", [1, 4, META])

        ring = st.enter_context(nc.psum_tensor("ring", [P, 2, BANK], F32))
        simp = st.enter_context(nc.psum_tensor("simp", [P, 2, D], F32))
        rout = st.enter_context(nc.psum_tensor("rout", [P, BANK], F32))
        lgp = rout[:, 0:BT * E].rearrange("p (t e) -> p t e", e=E)
        rkp = rout[:, BT * E:2 * BT * E].rearrange("p (t e) -> p t e", e=E)
        totp = rout[:, 2 * BT * E:2 * BT * E + E]

        s_const = sem("s_const")
        s_pool = sem("s_pool")
        s_mask = sem("s_mask")
        s_init = sem("s_init")
        s_ctx = sem("s_ctx")
        s_xin = [sem(f"s_xin{i}") for i in range(UNITS)]
        s_ring = sem("s_ring")
        s_ev = sem("s_ev")
        s_pn = sem("s_pn")
        s_mva = sem("s_mva")
        s_rsa = sem("s_rsa")
        s_sim = sem("s_sim")
        s_mvs = sem("s_mvs")
        s_rss = sem("s_rss")
        s_z1 = sem("s_z1")
        s_nmx = sem("s_nmx")
        s_exp = sem("s_exp")
        s_x1 = sem("s_x1")
        s_mvb = sem("s_mvb")
        s_rsb = sem("s_rsb")
        s_x2 = sem("s_x2")
        s_st = [sem(f"s_st{i}") for i in range(2)]
        s_lg = sem("s_lg")
        s_lgr = sem("s_lgr")
        s_pe = sem("s_pe")
        s_both = sem("s_both")
        s_rk = sem("s_rk")
        s_rec = sem("s_rec")
        s_row = sem("s_row")
        s_scat = sem("s_scat")
        s_dv = sem("s_dv")
        s_pq = sem("s_pq")

        xr = x.rearrange("b (t p) d -> (b t) p d", p=P)
        outr = x1_out.rearrange("b (t p) d -> (b t) p d", p=P)
        x2r = x2_rows[0:T, :].rearrange("(t p) d -> t p d", p=P)
        block = st.enter_context(nc.Block())

        @block.sync
        def _(sp):
            sp.dma_start(wk_in[:, :, :], W_k.rearrange("(a p) c -> p a c", p=P)).then_inc(s_const, 16)
            sp.dma_start(bk_row[:, :], b_k.rearrange("(a n) -> a n", a=1)).then_inc(s_const, 16)
            sp.dma_start(gam[:, :], gamma.partition_broadcast(P)).then_inc(s_const, 16)
            sp.dma_start(bet[:, :], beta.partition_broadcast(P)).then_inc(s_const, 16)
            sp.dma_start(gw[:, :, :], gate_w.rearrange("(k p) e -> p k e", p=P)).then_inc(s_const, 16)
            with sp.Fori(0, BATCH) as b:
                sp.wait_ge(s_ev, b * RING_B)
                sp.dma_start(ctxt[:, :, :],
                             ctx_in[bass.ds(b, 1)].rearrange("b (t p) c -> p (b t) c", p=P)).then_inc(s_ctx, 16)
                for u in range(UNITS):
                    sp.wait_ge(s_x1, b * BT)
                    sp.dma_start(xin[:, u, :, :], xr[bass.ds(b * BT + u * UNIT, UNIT)].rearrange(
                        "t p d -> p t d")).then_inc(s_xin[u], 16)
                for t in range(BT):
                    sp.wait_ge(s_x1, b * BT + t + 1)
                    sp.dma_start(outr[bass.ds(b * BT + t, 1)].rearrange("t p d -> (t p) d"),
                                 x1[:, t % 2, :]).then_inc(s_st[t % 2], 16)
                    sp.wait_ge(s_x2, b * BT + t + 1)
                    sp.dma_start(x2r[bass.ds(b * BT + t, 1)].rearrange("t p d -> (t p) d"),
                                 x2[:, t % 2, :]).then_inc(s_st[t % 2], 16)
            for i in range(2):
                sp.wait_ge(s_st[i], BATCH * BT // 2 * 32)

        @block.gpsimd
        def _(pool):
            step = Chain(pool, s_pool, 0, 14)
            nc.gpsimd.memset(leps[:, :], LN_EPS).then_inc(s_mask, 1)
            nc.gpsimd.memset(seps[:, :], SIM_EPS / SIM_SCALE ** 2).then_inc(s_mask, 1)
            nc.gpsimd.memset(onesm[:, :], 1.0).then_inc(s_mask, 1)
            nc.gpsimd.memset(zrow[:, :], 0.0).then_inc(s_mask, 1)
            nc.gpsimd.memset(ones_row[:, :], 1.0).then_inc(s_mask, 1)
            nc.gpsimd.memset(mhalf[:, :], -0.5).then_inc(s_mask, 1)
            step(nc.gpsimd.memset(ident[:, :], 1.0))
            step(nc.gpsimd.affine_select(out=ident[:, :], in_=ident[:, :], compare_op=ALU.is_equal, fill=0.0,
                                         base=0, pattern=[[1, P]], channel_multiplier=-1))
            step(nc.gpsimd.memset(before[:, :], 1.0))
            step(nc.gpsimd.affine_select(out=before[:, :], in_=before[:, :], compare_op=ALU.is_gt, fill=0.0,
                                         base=0, pattern=[[1, P]], channel_multiplier=-1))
            step(nc.gpsimd.iota(pref[:, :], [[-1, E]], base=E, channel_multiplier=0))
            step(nc.gpsimd.tensor_copy(preff[:, :], pref[:, :]))
            step(nc.gpsimd.tensor_scalar(eidf[:, :], preff[:, :], -1.0, float(E), ALU.mult, ALU.add))
            step(nc.gpsimd.tensor_scalar(ebase[:, :], eidf[:, :], float(LIST), None, ALU.mult))
            step(nc.gpsimd.tensor_copy(lbase[:, :], ebase[:, :]))
            step(nc.gpsimd.iota(rowid[:, :], [[P, BT]], base=0, channel_multiplier=1))
            step(nc.gpsimd.iota(seqs[:, :], [[0, BT]], base=SEQ, channel_multiplier=0))
            step(nc.gpsimd.iota(sidx[:, :, :], [[1, META], [0, E]], base=0, channel_multiplier=0))
            step(nc.gpsimd.iota(empty[:, :, 0:1], [[0, TAB // P], [0, 1]], base=NOROW, channel_multiplier=0))
            step(nc.gpsimd.iota(empty[:, :, 1:2], [[0, TAB // P], [0, 1]], base=0, channel_multiplier=0))
            step.close()
            pool.dma_start(table.rearrange("(p n) c -> p (n c)", p=P),
                           empty[:, :, :].rearrange("p n c -> p (n c)")).then_inc(s_init, 16)
            pool.wait_ge(s_mask, 6)
            pool.dma_start(x2_rows[T:T + 1, :], zrow[:, :]).then_inc(s_init, 16)
            pool.wait_ge(s_init, 32)
            with pool.Fori(0, BATCH) as b:
                step = Chain(pool, s_pq, b * (UNITS * (1 + UNIT * 2)), UNITS * (1 + UNIT * 2))

                def sim_rstd(t):
                    pool.wait_ge(s_mvs, b * BT + t + 1)
                    step(nc.gpsimd.tensor_tensor(ve[:, 4 + t % 2:5 + t % 2], mv_s[:, t % 2, 1:2], seps[:, :],
                                                 ALU.add))
                    nc.gpsimd.tensor_tensor(rs_s[:, t % 2:t % 2 + 1], ve[:, 4 + t % 2:5 + t % 2], mhalf[:, 0:1],
                                            ALU.pow).then_inc(s_rss, 1)

                def row_rstd(t):
                    pool.wait_ge(s_mvb, b * BT + t + 1)
                    step(nc.gpsimd.tensor_tensor(ve[:, 8 + t % 2:9 + t % 2], mv_b[:, t % 2, 1:2], leps[:, 0:1],
                                                 ALU.add))
                    nc.gpsimd.tensor_tensor(rs_b[:, t % 2:t % 2 + 1], ve[:, 8 + t % 2:9 + t % 2], mhalf[:, 0:1],
                                            ALU.pow).then_inc(s_rsb, 1)

                for u in range(UNITS):
                    pool.wait_ge(s_mva, b * UNITS + u + 1)
                    step(nc.gpsimd.tensor_tensor(ve[:, 0:UNIT], mv_a[:, :, 1], leps[:, :], ALU.add))
                    nc.gpsimd.tensor_tensor(rs_a[:, :], ve[:, 0:UNIT], mhalf[:, :], ALU.pow).then_inc(s_rsa, 1)
                    for what, t in SCHEDULE:
                        if what == "stats":
                            sim_rstd(u * UNIT + t)
                        elif what == "x1":
                            row_rstd(u * UNIT + t)
                step.close()
                pool.wait_ge(s_rec, b + 1)
                nc.gpsimd.tensor_tensor(rowid[:, :], rowid[:, :], seqs[:, :], ALU.add).then_inc(s_row, 1)
                for c in range(2):
                    for t in range(BT):
                        pool.indirect_dma_start(
                            out=table, out_offset=bass.IndirectOffsetOnAxis(ap=posi[:, c, t:t + 1], axis=0),
                            in_=rec[:, c, t, :], in_offset=None).then_inc(s_scat, 16)
            pool.wait_ge(s_scat, BATCH * 2 * BT * 16)

        @block.tensor
        def _(pe):
            pe.wait_ge(s_pool, 2)
            pe.wait_ge(s_mask, 6)
            pe.wait_ge(s_const, 80)
            for dc in range(2):
                for c in range(2):
                    mm = pe.transpose(ring[:, dc, c * P:(c + 1) * P], wk_in[:, dc, c * P:(c + 1) * P], ident[:, :])
                mm.then_inc(s_ring, 1)
            with pe.Fori(0, BATCH) as b:
                g0 = b * RING_B + RING_PRE
                n = 0
                pe.wait_ge(s_ctx, 16 * b + 16)
                for c in range(2):
                    for jh in range(2):
                        pe.wait_ge(s_ev, g0 + n - 1)
                        for j in range(4):
                            mm = pe.transpose(ring[:, n % 2, j * P:(j + 1) * P],
                                              ctxt[:, jh * 4 + j, c * P:(c + 1) * P], ident[:, :])
                        mm.then_inc(s_ring, 1)
                        n += 1
                for dc in range(2):
                    for jh in range(2):
                        pe.wait_ge(s_ev, g0 + max(n - 1, 4))
                        o = ring[:, n % 2, :]
                        for c in range(2):
                            pe.matmul(o, wkT[:, c, dc * P:(dc + 1) * P], ctxT[:, c, jh * BANK:(jh + 1) * BANK],
                                      start=(c == 0), stop=False)
                        pe.matmul(o, bk_row[:, dc * P:(dc + 1) * P], ones_row[:, :], start=False,
                                  stop=True).then_inc(s_ring, 1)
                        n += 1
                for q in range(BT // 2):
                    pe.wait_ge(s_ev, g0 + n - 1)
                    for h in range(2):
                        o = ring[:, n % 2, h * CD:(h + 1) * CD]
                        jt = 2 * q + h
                        for c in range(2):
                            pe.matmul(o, ctxT[:, c, jt * P:(jt + 1) * P], wkT[:, c, :], start=(c == 0), stop=False)
                        mm = pe.matmul(o, ones_row[:, 0:P], bk_row[:, :], start=False, stop=True)
                    mm.then_inc(s_ring, 1)
                    n += 1

                for u in range(UNITS):
                    for t in range(UNIT):
                        pe.wait_ge(s_pn, b * BT + u * UNIT + t + 1)
                        for h in range(2):
                            pe.wait_ge(s_ev, g0 + n - 1)
                            for j in range(4):
                                k = 4 * h + j
                                mm = pe.transpose(ring[:, n % 2, j * P:(j + 1) * P],
                                                  pn[:, t % 2, k * P:(k + 1) * P], ident[:, :])
                            mm.then_inc(s_ring, 1)
                            n += 1
                    filled = n
                    for dc in range(2):
                        pe.wait_ge(s_ev, g0 + filled)
                        for k in range(KT):
                            mm = pe.matmul(ring[:, n % 2, :], kv[:, k, dc * P:(dc + 1) * P], pT[:, k, :],
                                           start=(k == 0), stop=(k == KT - 1))
                        mm.then_inc(s_ring, 1)
                        n += 1
                    pe.wait_ge(s_ev, g0 + n)

                    def sim(t):
                        pe.wait_ge(s_z1, b * BT + t - 1 if t >= 2 else b * BT)
                        for h in range(2):
                            for dc in range(2):
                                mm = pe.matmul(simp[:, t % 2, h * BANK:(h + 1) * BANK],
                                               oT[:, dc, (t % UNIT) * P:(t % UNIT + 1) * P],
                                               kvT[:, dc, h * BANK:(h + 1) * BANK], start=(dc == 0), stop=(dc == 1))
                        mm.then_inc(s_sim, 1)

                    sim(u * UNIT)
                    sim(u * UNIT + 1)
                    for t in range(u * UNIT, u * UNIT + UNIT):
                        if t % UNIT + 2 < UNIT:
                            sim(t + 2)
                        pe.wait_ge(s_x2, b * BT + t + 1)
                        for h in range(2):
                            pe.wait_ge(s_ev, g0 + n - 1)
                            for j in range(4):
                                k = 4 * h + j
                                mm = pe.transpose(ring[:, n % 2, j * P:(j + 1) * P],
                                                  x2[:, t % 2, k * P:(k + 1) * P], ident[:, :])
                            mm.then_inc(s_ring, 1)
                            n += 1
                        if t == 0:
                            pe.wait_ge(s_rec, b)
                        pe.wait_ge(s_ev, g0 + n)
                        for k in range(KT):
                            mm = pe.matmul(lgp[:, t, :], x2T[:, t % 2, k, :], gw[:, k, :], start=(k == 0),
                                           stop=(k == KT - 1))
                        mm.then_inc(s_lg, 1)
                assert n == RING_B
                pe.wait_ge(s_both, b + 1)
                for t in range(BT):
                    for q in range(t + 1):
                        pe.matmul(rkp[:, t, :], before[:, :] if q == t else onesm[:, :], both[:, q, :],
                                  start=(q == 0), stop=(q == t))
                for t in range(BT):
                    mm = pe.matmul(totp, onesm[:, :], both[:, t, :], start=(t == 0), stop=(t == BT - 1))
                mm.then_inc(s_rk, 1)

        @block.scalar
        def _(act):
            def put(out, in_):
                nc.scalar.activation(out, in_, ACT.Copy).then_inc(s_ev, 1)

            for dc in range(2):
                act.wait_ge(s_ring, dc + 1)
                put(wkT[:, :, dc * P:(dc + 1) * P], ring[:, dc, 0:2 * P].rearrange("p (c j) -> p c j", c=2))
            with act.Fori(0, BATCH) as b:
                g0 = b * RING_B + RING_PRE
                n = 0
                for c in range(2):
                    for jh in range(2):
                        act.wait_ge(s_ring, g0 + n + 1)
                        put(ctxT[:, c, jh * BANK:(jh + 1) * BANK], ring[:, n % 2, :])
                        n += 1
                for dc in range(2):
                    for jh in range(2):
                        act.wait_ge(s_ring, g0 + n + 1)
                        put(kvT[:, dc, jh * BANK:(jh + 1) * BANK], ring[:, n % 2, :])
                        n += 1
                for q in range(BT // 2):
                    act.wait_ge(s_ring, g0 + n + 1)
                    put(kv[:, 2 * q:2 * q + 2, :], ring[:, n % 2, :].rearrange("p (h c) -> p h c", h=2))
                    n += 1
                for u in range(UNITS):
                    for t in range(UNIT):
                        for h in range(2):
                            act.wait_ge(s_ring, g0 + n + 1)
                            put(pT[:, 4 * h:4 * h + 4, t * P:(t + 1) * P],
                                ring[:, n % 2, :].rearrange("p (k i) -> p k i", k=4))
                            n += 1
                    for dc in range(2):
                        act.wait_ge(s_ring, g0 + n + 1)
                        put(oT[:, dc, :], ring[:, n % 2, :])
                        n += 1

                    for what, t in SCHEDULE:
                        t += u * UNIT
                        if what == "scores":
                            act.wait_ge(s_nmx, b * BT + t + 1)
                            nc.scalar.activation(z[:, t % 2, :], z[:, t % 2, :], ACT.Exp, bias=nmx[:, t % 2:t % 2 + 1],
                                                 accum_out=esum[:, t % 2:t % 2 + 1]).then_inc(s_exp, 1)
                        elif what == "x2":
                            for h in range(2):
                                act.wait_ge(s_ring, g0 + n + 1)
                                put(x2T[:, t % 2, 4 * h:4 * h + 4, :],
                                    ring[:, n % 2, :].rearrange("p (k i) -> p k i", k=4))
                                n += 1
                act.wait_ge(s_lgr, b + 1)
                nc.scalar.activation(pr[:, :, :], lg[:, :, :], ACT.Exp).then_inc(s_pe, 1)

        @block.vector
        def _(dve):
            V = nc.vector
            dve.wait_ge(s_pool, 14)
            dve.wait_ge(s_const, 80)
            with dve.Fori(0, BATCH) as b:
                step = Chain(dve, s_dv, b * DV_STEPS, DV_STEPS)

                def stats(t):
                    dve.wait_ge(s_sim, b * BT + t + 1)
                    V.bn_stats(st_s[:, t % 2, 0, :], simp[:, t % 2, 0:BANK])
                    V.bn_stats(st_s[:, t % 2, 1, :], simp[:, t % 2, BANK:D])
                    dve.drain()
                    V.bn_aggr(mv_s[:, t % 2, :], st_s[:, t % 2, :, :].rearrange("p a s -> p (a s)")
                              ).then_inc(s_mvs, 1)

                def scores(t):
                    dve.wait_ge(s_mvs, b * BT + t + 1)
                    zt = z[:, t % 2, :]
                    V.scalar_tensor_tensor(out=zt, in0=simp[:, t % 2, :], scalar=mv_s[:, t % 2, 0:1], in1=gam[:, :],
                                           op0=ALU.subtract, op1=ALU.mult).then_inc(s_z1, 1)
                    dve.wait_ge(s_rss, b * BT + t + 1)
                    dve.wait_ge(s_z1, b * BT + t + 1)
                    step(V.scalar_tensor_tensor(out=zt, in0=zt, scalar=rs_s[:, t % 2:t % 2 + 1], in1=bet[:, :],
                                                op0=ALU.mult, op1=ALU.add))
                    V.tensor_reduce(nmx[:, t % 2:t % 2 + 1], zt, AX.X, ALU.max, negate=True).then_inc(s_nmx, 1)

                def x1_tile(u, t):
                    g = u * UNIT + t
                    dve.wait_ge(s_exp, b * BT + g + 1)
                    step(V.reciprocal(rsum[:, g % 2:g % 2 + 1], esum[:, g % 2:g % 2 + 1]))
                    if g >= 2:
                        dve.wait_ge(s_st[g % 2], b * (BT // 2 * 32) + 32 * (g // 2))
                    else:
                        dve.wait_ge(s_st[g % 2], b * (BT // 2 * 32))
                    V.scalar_tensor_tensor(out=x1[:, g % 2, :], in0=z[:, g % 2, :], scalar=rsum[:, g % 2:g % 2 + 1],
                                           in1=xin[:, u, t, :], op0=ALU.mult, op1=ALU.add).then_inc(s_x1, 1)
                    dve.wait_ge(s_x1, b * BT + g + 1)
                    V.bn_stats(st_b[:, g % 2, 0, :], x1[:, g % 2, 0:BANK])
                    V.bn_stats(st_b[:, g % 2, 1, :], x1[:, g % 2, BANK:D])
                    dve.drain()
                    V.bn_aggr(mv_b[:, g % 2, :], st_b[:, g % 2, :, :].rearrange("p a s -> p (a s)")
                              ).then_inc(s_mvb, 1)

                def x2_tile(g):
                    dve.wait_ge(s_mvb, b * BT + g + 1)
                    dve.wait_ge(s_rsb, b * BT + g + 1)
                    dve.wait_ge(s_lg, b * BT + max(g - 1, 0))
                    V.tensor_scalar(x2[:, g % 2, :], x1[:, g % 2, :], mv_b[:, g % 2, 0:1], rs_b[:, g % 2:g % 2 + 1],
                                    ALU.subtract, ALU.mult).then_inc(s_x2, 1)

                for u in range(UNITS):
                    dve.wait_ge(s_xin[u], b * 16 + 16)
                    for t in range(UNIT):
                        V.bn_stats(st_a[:, t, 0, :], xin[:, u, t, 0:BANK])
                        V.bn_stats(st_a[:, t, 1, :], xin[:, u, t, BANK:D])
                    dve.drain()
                    for t in range(UNIT):
                        last = V.bn_aggr(mv_a[:, t, :], st_a[:, t, :, :].rearrange("p a s -> p (a s)"))
                    last.then_inc(s_mva, 1)
                    dve.wait_ge(s_mva, b * UNITS + u + 1)
                    dve.wait_ge(s_rsa, b * UNITS + u + 1)
                    for t in range(UNIT):
                        g = 12 + u * 18 + 2 * t - 4 + RING_PRE
                        if t >= 2:
                            dve.wait_ge(s_ring, b * RING_B + g + 2)
                        elif u == 1:
                            dve.wait_ge(s_ring, b * RING_B + 12 + 8 + RING_PRE)
                        else:
                            dve.wait_ge(s_ring, b * RING_B)
                        V.tensor_scalar(pn[:, t % 2, :], xin[:, u, t, :], mv_a[:, t, 0:1], rs_a[:, t:t + 1],
                                        ALU.subtract, ALU.mult).then_inc(s_pn, 1)
                    for what, t in SCHEDULE:
                        if what == "stats":
                            stats(u * UNIT + t)
                        elif what == "scores":
                            scores(u * UNIT + t)
                        elif what == "x1":
                            x1_tile(u, t)
                        else:
                            x2_tile(u * UNIT + t)

                def wide(a):
                    return a.unsqueeze(2).to_broadcast([P, BT, E])

                def pref_b():
                    return preff[:, :].unsqueeze(1).to_broadcast([P, BT, E])

                dve.wait_ge(s_lg, b * BT + BT)
                step(V.tensor_reduce(m1[:, :], lgp, AX.X, ALU.max))
                V.tensor_tensor(lg[:, :, :], lgp, wide(m1[:, :]), ALU.subtract).then_inc(s_lgr, 1)
                dve.wait_ge(s_pe, b + 1)
                step(V.tensor_reduce(msum[:, :], pr[:, :, :], AX.X, ALU.add))
                step(V.reciprocal(m2[:, :], msum[:, :]))
                step(V.tensor_tensor(pr[:, :, :], pr[:, :, :], wide(m2[:, :]), ALU.mult))

                def choose(top, onehot):
                    step(V.tensor_reduce(top, pr[:, :, :], AX.X, ALU.max))
                    step(V.tensor_tensor(t0[:, :, :], pr[:, :, :], wide(top), ALU.is_equal))
                    step(V.tensor_tensor(t0[:, :, :], t0[:, :, :], pref_b(), ALU.mult))
                    step(V.tensor_reduce(mk[:, :], t0[:, :, :], AX.X, ALU.max))
                    step(V.tensor_tensor(onehot, t0[:, :, :], wide(mk[:, :]), ALU.is_equal))

                choose(m1[:, :], oh1[:, :, :])
                step(V.scalar_tensor_tensor(out=pr[:, :, :], in0=oh1[:, :, :], scalar=-2.0, in1=pr[:, :, :],
                                            op0=ALU.mult, op1=ALU.add))
                choose(m2[:, :], oh2[:, :, :])
                V.tensor_tensor(both[:, :, :], oh1[:, :, :], oh2[:, :, :], ALU.add).then_inc(s_both, 1)
                step(V.tensor_tensor(msum[:, :], m1[:, :], m2[:, :], ALU.add))
                step(V.reciprocal(mk[:, :], msum[:, :]))
                dve.wait_ge(s_scat, b * (2 * BT * 16))
                dve.wait_ge(s_row, b)
                for c, top in enumerate((m1, m2)):
                    V.tensor_tensor(rec[:, c, :, 1].bitcast(F32), top[:, :], mk[:, :], ALU.mult)
                    step(V.tensor_copy(rec[:, c, :, 0], rowid[:, :]))
                dve.wait_ge(s_rk, b + 1)
                step(V.tensor_tensor(t0[:, :, :], rkp, lbase[:, :].unsqueeze(1).to_broadcast([P, BT, E]), ALU.add))
                for c, oh in enumerate((oh1, oh2)):
                    step(V.tensor_tensor(oh[:, :, :], oh[:, :, :], t0[:, :, :], ALU.mult))
                    step(V.tensor_reduce(posf[:, c, :], oh[:, :, :], AX.X, ALU.add))
                step(V.tensor_tensor(lbase[:, :], lbase[:, :], totp, ALU.add))
                V.tensor_copy(posi[:, :, :], posf[:, :, :]).then_inc(s_rec, 1)
                step.close()

            step = Chain(dve, s_dv, BATCH * DV_STEPS, 38)
            cnt, has, blk, nsl, two, end, beg, th = (c8[:, i, :] for i in range(8))
            tmp, tm2 = c8[:, 8, :], c8[:, 9, :]
            step(V.tensor_tensor(cnt, lbase[:, :], ebase[:, :], ALU.subtract))
            step(V.tensor_scalar(has, cnt, 1.0, None, ALU.min))
            step(V.tensor_scalar(i8[:, 0, :], cnt, float(P - 1), None, ALU.add))
            step(V.tensor_scalar(i8[:, 1, :], i8[:, 0, :], 7, None, ALU.logical_shift_right))
            step(V.tensor_copy(tmp, i8[:, 1, :]))
            step(V.tensor_scalar(tmp, tmp, 2.0, None, ALU.max))
            step(V.tensor_tensor(blk, tmp, has, ALU.mult))
            step(V.tensor_scalar(i8[:, 0, :], blk, 2.0, 86.0, ALU.add, ALU.mult))
            step(V.tensor_scalar(i8[:, 1, :], i8[:, 0, :], 8, None, ALU.logical_shift_right))
            step(V.tensor_copy(nsl, i8[:, 1, :]))
            step(V.scalar_tensor_tensor(out=two, in0=nsl, scalar=3.0, in1=blk, op0=ALU.mult, op1=ALU.subtract))
            step(V.tensor_tensor(th, nsl, two, ALU.subtract))
            step(V.tensor_copy(tmp, nsl))
            step(V.tensor_copy(tm2[:, 0:1], tmp[:, 0:1]))
            step(V.tensor_tensor(tm2[:, 1:E], tmp[:, 1:E], tmp[:, 0:E - 1], ALU.add))
            step(V.tensor_copy(tmp[:, 0:2], tm2[:, 0:2]))
            step(V.tensor_tensor(tmp[:, 2:E], tm2[:, 2:E], tm2[:, 0:E - 2], ALU.add))
            step(V.tensor_copy(end[:, 0:4], tmp[:, 0:4]))
            step(V.tensor_tensor(end[:, 4:E], tmp[:, 4:E], tmp[:, 0:E - 4], ALU.add))
            step(V.tensor_tensor(beg, end, nsl, ALU.subtract))

            def by_slot(a):
                return a[0:1, :].unsqueeze(1).to_broadcast([1, META, E])

            s_i, mine, i_in, over, t_a, t_b = (sl[:, i, :, :] for i in range(6))
            step(V.tensor_copy(s_i, sidx[:, :, :]))
            step(V.tensor_tensor(t_a, s_i, by_slot(beg), ALU.is_ge))
            step(V.tensor_tensor(t_b, s_i, by_slot(end), ALU.is_lt))
            step(V.tensor_tensor(mine, t_a, t_b, ALU.mult))
            step(V.tensor_tensor(i_in, s_i, by_slot(beg), ALU.subtract))
            step(V.tensor_tensor(over, i_in, by_slot(th), ALU.subtract))
            step(V.tensor_scalar(t_a, over, 0.0, float(-P), ALU.max, ALU.mult))
            step(V.scalar_tensor_tensor(out=t_a, in0=i_in, scalar=float(SB * P), in1=t_a, op0=ALU.mult, op1=ALU.add))
            step(V.tensor_tensor(t_a, t_a, by_slot(ebase[:, :]), ALU.add))
            step(V.tensor_tensor(t_a, t_a, mine, ALU.mult))
            step(V.tensor_reduce(metaf[:, 1, :], t_a, AX.X, ALU.add))
            step(V.tensor_scalar(t_b, over, 0.0, None, ALU.is_ge))
            step(V.tensor_scalar(t_b, t_b, -1.0, float(SB), ALU.mult, ALU.add))
            step(V.tensor_tensor(t_b, t_b, mine, ALU.mult))
            step(V.tensor_reduce(metaf[:, 3, :], t_b, AX.X, ALU.add))
            step(V.tensor_tensor(t_a, mine, by_slot(eidf[:, :]), ALU.mult))
            step(V.tensor_reduce(metaf[:, 0, :], t_a, AX.X, ALU.add))
            is3, pl = sl[:, 6, :, 0], sl[:, 7, :, 0]
            V.tensor_scalar(is3, metaf[:, 3, :], float(SB), None, ALU.is_equal)
            step(V.tensor_scalar(pl, metaf[:, 1, :], float(2 * P - PADROW), None, ALU.add))
            V.tensor_tensor(pl, pl, is3, ALU.mult).then_inc(s_dv, 1)
            dve.wait_ge(s_dv, BATCH * DV_STEPS + 39)
            V.tensor_scalar(metaf[:, 2, :], pl, float(PADROW), None, ALU.add).then_inc(s_dv, 1)
            dve.wait_ge(s_dv, BATCH * DV_STEPS + 40)
            V.tensor_copy(meta[:, :, :], metaf[:, :, :]).then_inc(s_dv, 1)
            step.close()


SCHEDULE = [("stats", 0), ("stats", 1), ("scores", 0), ("scores", 1), ("x1", 0), ("stats", 2), ("x2", 0),
            ("scores", 2), ("x1", 1), ("stats", 3), ("x2", 1), ("scores", 3), ("x1", 2), ("x2", 2), ("x1", 3),
            ("x2", 3)]
DV_STEPS = 2 * BT + 1 + 3 + 5 + 1 + 5 + 2 + 2 + 1 + 4 + 1


def experts(nc, w1, w3, w2, out, x2_rows, table, meta):
    STEP4 = MT // 4 - 1
    with ExitStack() as st:
        def sb(name, shape, dt=F32):
            return st.enter_context(nc.sbuf_tensor(name, shape, dt))

        def sem(name):
            return st.enter_context(nc.semaphore(name))

        raw13 = [sb(f"raw13_{i}", [P, 2, KT, 2 * P]) for i in range(2)]
        raw2 = [sb(f"raw2_{i}", [P, 2, D]) for i in range(2)]
        hi13 = [sb(f"hi13_{i}", [P, 2, KT, P], F32R) for i in range(2)]
        lo13 = [sb(f"lo13_{i}", [P, 2, KT, P], F32R) for i in range(2)]
        hi2 = [sb(f"hi2_{i}", [P, D], F32R) for i in range(2)]
        lo2 = [sb(f"lo2_{i}", [P, D], F32R) for i in range(2)]
        xg = sb("xg", [P, SB, D])
        xhi = sb("xhi", [P, KT, SB * P], F32R)
        xlo = sb("xlo", [P, KT, SB * P], F32R)
        sil = sb("sil", [P, SB * P])
        hid = sb("hid", [P, SB * P])
        hhi = [sb(f"hhi_{i}", [P, SB * P], F32R) for i in range(2)]
        hlo = [sb(f"hlo_{i}", [P, SB * P], F32R) for i in range(2)]
        y = sb("y", [P, SB, D])
        id_g = sb("id_g", [P, SB, 2], I32)
        id_s = sb("id_s", [P, SB, 2], I32)
        ident = sb("ident2", [P, P])
        ticks = sb("ticks", [P, 2])

        p1 = st.enter_context(nc.psum_tensor("p1", [P, BANK], F32))
        p3 = st.enter_context(nc.psum_tensor("p3", [P, BANK], F32))
        acc = st.enter_context(nc.psum_tensor("acc", [P, SB, D], F32))

        s_raw13 = [sem(f"s_raw13_{i}") for i in range(2)]
        s_raw2 = [sem(f"s_raw2_{i}") for i in range(2)]
        s_hi13 = sem("s_hi13")
        s_lo13 = sem("s_lo13")
        s_hi2 = sem("s_hi2")
        s_lo2 = sem("s_lo2")
        s_h1 = sem("s_h1")
        s_h3 = sem("s_h3")
        s_sil = sem("s_sil")
        s_hid = sem("s_hid")
        s_hhi = sem("s_hhi")
        s_hlo = sem("s_hlo")
        s_out = sem("s_out")
        s_t = sem("s_t")
        s_thi = sem("s_thi")
        s_tlo = sem("s_tlo")
        s_ya = sem("s_ya")
        s_yd = sem("s_yd")
        s_idg = sem("s_idg")
        s_ids = sem("s_ids")
        s_xg = sem("s_xg")
        s_sc = sem("s_sc")
        s_id = sem("s_id")
        s_tick = sem("s_tick")

        out_rows = out.rearrange("b s d -> (b s) d")
        w1v = w1.rearrange("e (k p) m -> e p k m", p=P)
        w3v = w3.rearrange("e (k p) m -> e p k m", p=P)
        w2v = w2.rearrange("e (m p) d -> e p m d", p=P)
        block = st.enter_context(nc.Block())

        def slot_value(eng, row, s, most):
            return eng.value_load(meta[0:1, row, bass.ds(s, 1)], min_val=0, max_val=most)

        @block.sync
        def _(sp):
            def load(e, pair, parity, s):
                if not (isinstance(pair, int) and pair == 0 and isinstance(s, int)):
                    sp.wait_ge(s_lo13, s * MT + pair * 2 - 2)
                sp.dma_start(raw13[parity][:, 0], w1v[bass.ds(e, 1), :, :, bass.ds(pair * 2 * P, 2 * P)].rearrange(
                    "e p k m -> (e p) k m")).then_inc(s_raw13[parity], 16)
                sp.dma_start(raw13[parity][:, 1], w3v[bass.ds(e, 1), :, :, bass.ds(pair * 2 * P, 2 * P)].rearrange(
                    "e p k m -> (e p) k m")).then_inc(s_raw13[parity], 16)
                if not (isinstance(pair, int) and pair == 0 and isinstance(s, int)):
                    sp.wait_ge(s_lo2, s * MT + pair * 2 - 2)
                sp.dma_start(raw2[parity][:, :, :], w2v[bass.ds(e, 1), :, bass.ds(pair * 2, 2), :].rearrange(
                    "e p m d -> (e p) m d")).then_inc(s_raw2[parity], 16)

            e0 = slot_value(sp, 0, 0, E - 1)
            load(e0, 0, 0, 0)
            with sp.Fori(0, SLOTS) as s:
                nb = slot_value(sp, 3, s, SB)
                with sp.If(nb >= 2):
                    e = slot_value(sp, 0, s, E - 1)
                    with sp.Fori(0, MT // 4 - 1) as i:
                        load(e, i * 2 + 1, 1, s)
                        load(e, i * 2 + 2, 0, s)
                    load(e, MT // 2 - 1, 1, s)
                nxt = slot_value(sp, 3, s + 1, SB)
                with sp.If(nxt >= 2):
                    e = slot_value(sp, 0, s + 1, E - 1)
                    load(e, 0, 0, s + 1)

        @block.scalar
        def _(act):
            def split13(s, fills, par4):
                j, half = par4 // 2, par4 % 2
                act.wait_ge(s_raw13[j], (s * (MT // 4) + fills) * 32)
                nc.scalar.activation(hi13[par4 % 2][:, :, :, :].rearrange("p a k c -> p (a k) c"),
                                     raw13[j][:, :, :, half * P:(half + 1) * P].rearrange("p a k c -> p (a k) c"),
                                     ACT.Copy).then_inc(s_hi13, 1)

            def tile(s, base, q, quad, last):
                g = s * MT + base
                if not last:
                    act.wait_ge(s_h3, g + q)
                    split13(s, quad + (1 if q == 3 else 0), (q + 1) % 4)
                act.wait_ge(s_h1, g + q + 1)
                act.wait_ge(s_hid, g + q)
                nc.scalar.activation(sil[:, :], p1[:, 0:SB * P], ACT.Silu).then_inc(s_sil, 1)
                act.wait_ge(s_raw2[q // 2], (s * (MT // 4) + quad) * 16)
                nc.scalar.activation(hi2[q % 2][:, :], raw2[q // 2][:, q % 2, :], ACT.Copy).then_inc(s_hi2, 1)
                act.wait_ge(s_hid, g + q + 1)
                nc.scalar.activation(hhi[q % 2][:, :], hid[:, :], ACT.Copy).then_inc(s_hhi, 1)

            def rows_split(n):
                for q in range(2 * SB):
                    blk, k = q // 2, 4 * (q % 2)
                    act.wait_ge(s_t, n * (2 * SB) + q + 1)
                    nc.scalar.activation(xhi[:, k:k + 4, blk * P:(blk + 1) * P],
                                         (p1, p3)[q % 2][:, :].rearrange("p (k i) -> p k i", k=4),
                                         ACT.Copy).then_inc(s_thi, 1)

            rows_split(0)
            split13(0, 1, 0)
            with act.Fori(0, SLOTS) as s:
                nb = slot_value(act, 3, s, SB)
                nxt = slot_value(act, 3, s + 1, SB)
                with act.If(nb >= 2):
                    with act.Fori(0, STEP4) as i:
                        for q in range(4):
                            tile(s, i * 4, q, i + 1, False)
                    for q in range(4):
                        tile(s, STEP4 * 4, q, STEP4 + 1, q == 3)
                    rows_split(s + 1)
                with act.If(nxt >= 2):
                    split13(s + 1, 1, 0)
                with act.If(nb >= 2):
                    act.wait_ge(s_ids, s * 32 + 32)
                    act.wait_ge(s_out, s + 1)
                    act.wait_ge(s_sc, s * (SB * 16))
                    for j in range(SB):
                        last = nc.scalar.activation(y[:, j, 0:BANK], acc[:, j, 0:BANK], ACT.Copy,
                                                    scale=id_s[:, j, 1:2].bitcast(F32))
                    last.then_inc(s_ya, 1)

        @block.vector
        def _(dve):
            V = nc.vector

            def split13(s, m, par4):
                j, half = par4 // 2, par4 % 2
                g = s * MT + m
                dve.wait_ge(s_hi13, g + 1)
                V.tensor_tensor(lo13[par4 % 2][:, :, :, :].rearrange("p a k c -> p (a k) c"),
                                raw13[j][:, :, :, half * P:(half + 1) * P].rearrange("p a k c -> p (a k) c"),
                                hi13[par4 % 2][:, :, :, :].rearrange("p a k c -> p (a k) c").bitcast(F32),
                                ALU.subtract).then_inc(s_lo13, 1)

            def tile(s, base, q, last):
                g = s * MT + base
                if not last:
                    split13(s, base + (q + 1), (q + 1) % 4)
                dve.wait_ge(s_h3, g + q + 1)
                dve.wait_ge(s_sil, g + q + 1)
                dve.wait_ge(s_hlo, g + q)
                V.tensor_tensor(hid[:, :], sil[:, :], p3[:, 0:SB * P], ALU.mult).then_inc(s_hid, 1)
                dve.wait_ge(s_hi2, g + q + 1)
                V.tensor_tensor(lo2[q % 2][:, :], raw2[q // 2][:, q % 2, :], hi2[q % 2][:, :].bitcast(F32),
                                ALU.subtract).then_inc(s_lo2, 1)
                dve.wait_ge(s_hhi, g + q + 1)
                V.tensor_tensor(hlo[q % 2][:, :], hid[:, :], hhi[q % 2][:, :].bitcast(F32),
                                ALU.subtract).then_inc(s_hlo, 1)

            def rows_split(n):
                for q in range(2 * SB):
                    blk, k = q // 2, 4 * (q % 2)
                    dve.wait_ge(s_thi, n * (2 * SB) + q + 1)
                    V.tensor_tensor(xlo[:, k:k + 4, blk * P:(blk + 1) * P],
                                    (p1, p3)[q % 2][:, :].rearrange("p (k i) -> p k i", k=4),
                                    xhi[:, k:k + 4, blk * P:(blk + 1) * P].bitcast(F32),
                                    ALU.subtract).then_inc(s_tlo, 1)

            rows_split(0)
            split13(0, 0, 0)
            with dve.Fori(0, SLOTS) as s:
                nb = slot_value(dve, 3, s, SB)
                nxt = slot_value(dve, 3, s + 1, SB)
                with dve.If(nb >= 2):
                    with dve.Fori(0, STEP4) as i:
                        for q in range(4):
                            tile(s, i * 4, q, False)
                    for q in range(4):
                        tile(s, STEP4 * 4, q, q == 3)
                    rows_split(s + 1)
                with dve.If(nxt >= 2):
                    split13(s + 1, 0, 0)
                with dve.If(nb >= 2):
                    dve.wait_ge(s_ids, s * 32 + 32)
                    dve.wait_ge(s_out, s + 1)
                    dve.wait_ge(s_sc, s * (SB * 16))
                    for j in range(SB):
                        last = V.tensor_scalar(y[:, j, BANK:D], acc[:, j, BANK:D], id_s[:, j, 1:2].bitcast(F32), None,
                                               ALU.mult)
                    last.then_inc(s_yd, 1)

        @block.tensor
        def _(pe):
            def hidden(s, m, par, nb, after_rows):
                g = s * MT + m
                n = nb * P
                pe.wait_ge(s_lo13, g + 1)
                if after_rows:
                    pe.wait_ge(s_tlo, s * (2 * SB) + 2 * SB)
                else:
                    pe.wait_ge(s_sil, g)
                for a, (bank, done) in enumerate(((p1, s_h1), (p3, s_h3))):
                    if a == 1 and not after_rows:
                        pe.wait_ge(s_hid, g)
                    for k in range(KT):
                        pe.matmul(bank[:, 0:n], hi13[par][:, a, k, :], xhi[:, k, 0:n], start=(k == 0), stop=False)
                        pe.matmul(bank[:, 0:n], hi13[par][:, a, k, :], xlo[:, k, 0:n], start=False, stop=False)
                        mm = pe.matmul(bank[:, 0:n], lo13[par][:, a, k, :], xhi[:, k, 0:n], start=False,
                                       stop=(k == KT - 1))
                    mm.then_inc(done, 1)

            def down(s, m, par, nb, first, last, blocks=None):
                g = s * MT + m
                pe.wait_ge(s_hlo, g + 1)
                pe.wait_ge(s_lo2, g + 1)
                for j in blocks if blocks is not None else range(nb):
                    for h in range(2):
                        o = acc[:, j, h * BANK:(h + 1) * BANK]
                        rows, cols = slice(j * P, (j + 1) * P), slice(h * BANK, (h + 1) * BANK)
                        pe.matmul(o, hhi[par][:, rows], hi2[par][:, cols], start=first, stop=False)
                        pe.matmul(o, hhi[par][:, rows], lo2[par][:, cols], start=False, stop=False)
                        mm = pe.matmul(o, hlo[par][:, rows], hi2[par][:, cols], start=False, stop=last)
                return mm

            def turn(n, q, first=False):
                blk, k = q // 2, 4 * (q % 2)
                if q == 0:
                    pe.wait_ge(s_xg, n * (SB * 16) + SB * 16)
                if q >= 2:
                    pe.wait_ge(s_tlo, n * (2 * SB) + q - 1)
                elif not first:
                    pe.wait_ge((s_sil, s_hid)[q], n * MT)
                for j in range(4):
                    mm = pe.transpose((p1, p3)[q % 2][:, j * P:(j + 1) * P], xg[:, blk, (k + j) * P:(k + j + 1) * P],
                                      ident[:, :])
                mm.then_inc(s_t, 1)

            def slot(s, nb):
                hidden(s, 0, 0, nb, True)
                hidden(s, 1, 1, nb, False)
                pe.wait_ge(s_ya, s)
                pe.wait_ge(s_yd, s)
                down(s, 0, 0, nb, True, False)
                with pe.Fori(0, MT // 2 - 1) as i:
                    for j in range(2):
                        hidden(s, i * 2 + (2 + j), j, nb, False)
                        down(s, i * 2 + (1 + j), 1 - j, nb, False, False)
                turn(s + 1, 0)
                turn(s + 1, 1)
                down(s, MT - 1, 1, nb, False, True, [0])
                turn(s + 1, 2)
                turn(s + 1, 3)
                mm = down(s, MT - 1, 1, nb, False, True, range(1, nb))
                mm.then_inc(s_out, 1)
                turn(s + 1, 4)
                turn(s + 1, 5)

            pe.wait_ge(s_id, 2)
            for h in range(2):
                for c in range(4):
                    pe.transpose(acc[:, SB - 1, h * BANK + c * P:h * BANK + (c + 1) * P], ident[:, :], ident[:, :])
            for q in range(2 * SB):
                turn(0, q, first=True)
            with pe.Fori(0, SLOTS) as s:
                nb = slot_value(pe, 3, s, SB)
                with pe.If(nb == 3):
                    slot(s, 3)
                with pe.If(nb == 2):
                    slot(s, 2)

        @block.gpsimd
        def _(pool):
            pool.memset(ident[:, :], 1.0).then_inc(s_id, 1)
            pool.wait_ge(s_id, 1)
            nc.gpsimd.affine_select(out=ident[:, :], in_=ident[:, :], compare_op=ALU.is_equal, fill=0.0,
                                    base=0, pattern=[[1, P]], channel_multiplier=-1).then_inc(s_id, 1)

            def records(s, to, done):
                place = slot_value(pool, 1, s, E * LIST)
                third = slot_value(pool, 2, s, E * LIST)
                pool.dma_start(to[:, 0:2, :], table[bass.ds(place, 2 * P), :].rearrange("(j p) c -> p j c", p=P)
                               ).then_inc(done, 16)
                pool.dma_start(to[:, 2, :], table[bass.ds(third, P), :]).then_inc(done, 16)

            def tick(n):
                pool.wait_ge(s_tick, n + 1)
                nc.gpsimd.tensor_tensor(ticks[:, 0:1], ticks[:, 0:1], ticks[:, 1:2], ALU.add).then_inc(s_tick, 1)

            def gather(n, ticked):
                records(n, id_g, s_idg)
                pool.wait_ge(s_idg, n * 32 + 32)
                tick(ticked)
                for j in range(SB):
                    pool.indirect_dma_start(out=xg[:, j, :], out_offset=None, in_=x2_rows,
                                            in_offset=bass.IndirectOffsetOnAxis(ap=id_g[:, j, 0:1], axis=0)
                                            ).then_inc(s_xg, 16)

            nc.gpsimd.memset(ticks[:, :], 0.0).then_inc(s_tick, 1)
            gather(0, 0)
            with pool.Fori(0, SLOTS) as s:
                nb = slot_value(pool, 3, s, SB)
                with pool.If(nb >= 2):
                    pool.wait_ge(s_t, s * (2 * SB) + 2 * SB)
                    pool.wait_ge(s_xg, s * (SB * 16) + SB * 16)
                    gather(s + 1, s * 2 + 1)
                    records(s, id_s, s_ids)
                    pool.wait_ge(s_ids, s * 32 + 32)
                    pool.wait_ge(s_ya, s + 1)
                    pool.wait_ge(s_yd, s + 1)
                    tick(s * 2 + 2)
                    for j in range(SB):
                        pool.indirect_dma_start(
                            out=out_rows, out_offset=bass.IndirectOffsetOnAxis(ap=id_s[:, j, 0:1], axis=0),
                            in_=y[:, j, :], in_offset=None, compute_op=ALU.add, bounds_check=T - 1,
                            oob_is_err=False).then_inc(s_sc, 16)
                    pool.wait_ge(s_sc, s * (SB * 16) + SB * 16)


def moe_kernel(nc, x, ctx_in, W_k, b_k, gamma, beta, gate_w, w1, w2, w3, out):
    x2_rows = nc.dram_tensor("x2_rows", [T + 1, D], F32, kind="Internal").ap()
    table = nc.dram_tensor("table", [TAB, 2], I32, kind="Internal").ap()
    with nc.sbuf_tensor("meta", [1, 4, META], I32) as meta:
        attend_and_route(nc, x, ctx_in, W_k, b_k, gamma, beta, gate_w, out, x2_rows, table, meta)
        experts(nc, w1, w3, w2, out, x2_rows, table, meta)


_INS = ['x', 'ctx_512', 'L0_xattn_W_k', 'L0_xattn_b_k', 'L0_xattn_ln_gamma', 'L0_xattn_ln_beta', 'L0_ffn_gate_w',
        'L0_ffn_w1', 'L0_ffn_w2', 'L0_ffn_w3']


def kernel(**inputs):
    import numpy as _np
    import concourse.bacc as _bacc
    from concourse.bass_utils import run_bass_kernel_spmd as _run

    nc = _bacc.Bacc("TRN2", target_bir_lowering=False, num_devices=1)
    arrays, args = {}, []
    for name in _INS:
        a = _np.ascontiguousarray(inputs[name])
        arrays[f"in_{name}"] = a
        args.append(nc.dram_tensor(f"in_{name}", a.shape, mybir.dt.from_np(a.dtype), kind="ExternalInput").ap())
    args.append(nc.dram_tensor("out_x", (BATCH, SEQ, D), F32, kind="ExternalOutput").ap())
    moe_kernel(nc, *args)
    r = _run(nc, [arrays], core_ids=[0])
    return r.results[0]["out_x"]
```

```python
import concourse.bass as bass
from concourse import mybir
from contextlib import ExitStack

F32 = mybir.dt.float32
F32R = mybir.dt.float32r
I32 = mybir.dt.int32
ALU = mybir.AluOpType
ACT = mybir.ActivationFunctionType
AX = mybir.AxisListType

P = 128
BATCH, SEQ, D = 4, 1024, 1024
CD = 256
E, M = 8, 3584
T = BATCH * SEQ
KT = D // P
MT = M // P
BANK = 512
UNIT = 4
UNITS = SEQ // (UNIT * P)
BT = SEQ // P
LIST = T
NOROW = T
SB = 3
PADROW = E * LIST
TAB = PADROW + 2 * BT * P
SLOTS = (2 * T // P + E + 2 * E) // SB
META = 32
META_STEPS = 47
GROUP = 32
WIDTHS = range(2 * P // GROUP, SB * P // GROUP + 1)
RING = 3
assert SLOTS < META
LN_EPS, SIM_EPS = 1e-5, 1e-6
SIM_SCALE = 1024 ** -0.5


class Chain:

    def __init__(self, eng, sem, base, per_pass):
        self.eng, self.sem, self.base, self.n, self.per_pass = eng, sem, base, 0, per_pass

    def __call__(self, ins):
        self.n += 1
        ins.then_inc(self.sem, 1)
        self.eng.wait_ge(self.sem, self.base + self.n)

    def close(self):
        assert self.n == self.per_pass, (self.n, self.per_pass)


def load_first(sp, first, w1, w3, w2, raw13, raw2, s_raw13, s_raw2):
    e = sp.value_load(first[0:1, 0:1], min_val=0, max_val=E - 1)
    for a, w in enumerate((w1, w3)):
        sp.dma_start(raw13[:, a], w[bass.ds(e, 1), :, 0:2 * P].rearrange("e (k p) m -> (e p) k m", p=P)
                     ).then_inc(s_raw13, 16)
    sp.dma_start(raw2[:, :, :], w2[bass.ds(e, 1), 0:2 * P, :].rearrange("e (m p) d -> (e p) m d", p=P)
                 ).then_inc(s_raw2, 16)


def attend_and_route(nc, x, ctx_in, W_k, b_k, gamma, beta, gate_w, x1_out, x2_rows, table, meta, first_weights):

    with ExitStack() as st:
        def sb(name, shape, dt=F32):
            return st.enter_context(nc.sbuf_tensor(name, shape, dt))

        def sem(name):
            return st.enter_context(nc.semaphore(name))

        xin = sb("xin", [P, UNITS, UNIT, D])
        ctxt = sb("ctxt", [P, BT, CD])
        wk_in = sb("wk_in", [P, 2, CD])
        wkT = sb("wkT", [P, 2, CD])
        bk_col = sb("bk_col", [P, 2])
        gam = sb("gam", [P, D])
        bet = sb("bet", [P, D])
        gw = sb("gw", [P, KT, E])
        ident = sb("ident", [P, P])
        onesm = sb("onesm", [P, P])
        before = sb("before", [P, P])
        ctxT = sb("ctxT", [P, 2, SEQ])
        kvT = sb("kvT", [P, 2, SEQ])
        kv = sb("kv", [P, BT, CD])
        pn = sb("pn", [P, 2, D])
        pT = sb("pT", [P, KT, UNIT * P])
        oT = sb("oT", [P, 2, UNIT * P])
        z = sb("z", [P, 2, D])
        x1 = sb("x1", [P, 2, D])
        x2 = sb("x2", [P, 2, D])
        x2T = sb("x2T", [P, 2, KT, P])
        st_a = sb("st_a", [P, UNIT, 2, 6])
        mv_a = sb("mv_a", [P, UNIT, 2])
        rs_a = sb("rs_a", [P, UNIT])
        st_s = sb("st_s", [P, 2, 2, 6])
        mv_s = sb("mv_s", [P, 2, 2])
        rs_s = sb("rs_s", [P, 2])
        st_b = sb("st_b", [P, 2, 2, 6])
        mv_b = sb("mv_b", [P, 2, 2])
        rs_b = sb("rs_b", [P, 2])
        ve = sb("ve", [P, 12])
        mhalf = sb("mhalf", [P, UNIT])
        leps = sb("leps", [P, UNIT])
        seps = sb("seps", [P, 1])
        nmx = sb("nmx", [P, 2])
        esum = sb("esum", [P, 2])
        rsum = sb("rsum", [P, 2])
        lg = sb("lg", [P, BT, E])
        pr = sb("pr", [P, BT, E])
        t0 = sb("t0", [P, BT, E])
        oh1 = sb("oh1", [P, BT, E])
        oh2 = sb("oh2", [P, BT, E])
        both = sb("both", [P, BT + 1, E])
        m1 = sb("m1", [P, BT])
        m2 = sb("m2", [P, BT])
        mk = sb("mk", [P, BT])
        msum = sb("msum", [P, BT])
        posf = sb("posf", [P, 2, BT])
        posi = sb("posi", [P, 2, BT], I32)
        rec = sb("rec", [P, 2, BT, 2], I32)
        rowid = sb("rowid", [P, BT], I32)
        seqs = sb("seqs", [P, BT], I32)
        pref = sb("pref", [P, E], I32)
        preff = sb("preff", [P, E])
        eidf = sb("eidf", [P, E])
        ebase = sb("ebase", [P, E])
        lbase = sb("lbase", [P, E])
        empty = sb("empty", [P, TAB // P, 2], I32)
        zrow = sb("zrow", [1, D])
        c8 = sb("c8", [P, 12, E])
        i8 = sb("i8", [P, 2, E], I32)
        sidx = sb("sidx", [1, META, E], I32)
        sl = sb("sl", [1, 8, META, E])
        im = sb("im", [1, 2, META], I32)
        first = sb("first", [1, 1], I32)
        metaf = sb("metaf", [1, 4, META])

        ring = st.enter_context(nc.psum_tensor("ring", [P, RING, BANK], F32))
        simp = st.enter_context(nc.psum_tensor("simp", [P, 2, D], F32))
        rout = st.enter_context(nc.psum_tensor("rout", [P, BANK], F32))
        lgp = rout[:, 0:BT * E].rearrange("p (t e) -> p t e", e=E)
        rkp = rout[:, BT * E:(2 * BT + 1) * E].rearrange("p (t e) -> p t e", e=E)

        s_wk = sem("s_wk")
        s_const = sem("s_const")
        s_gw = sem("s_gw")
        s_pool = sem("s_pool")
        s_mask = sem("s_mask")
        s_init = sem("s_init")
        s_ctx = sem("s_ctx")
        s_xin = [sem(f"s_xin{i}") for i in range(UNITS)]
        s_ring = sem("s_ring")
        s_ev = sem("s_ev")
        s_pn = sem("s_pn")
        s_mva = sem("s_mva")
        s_rsa = sem("s_rsa")
        s_sim = sem("s_sim")
        s_mvs = sem("s_mvs")
        s_rss = sem("s_rss")
        s_z1 = sem("s_z1")
        s_nmx = sem("s_nmx")
        s_exp = sem("s_exp")
        s_x1 = sem("s_x1")
        s_mvb = sem("s_mvb")
        s_rsb = sem("s_rsb")
        s_x2 = sem("s_x2")
        s_st = [sem(f"s_st{i}") for i in range(2)]
        s_lg = sem("s_lg")
        s_lgr = sem("s_lgr")
        s_pe = sem("s_pe")
        s_both = sem("s_both")
        s_rk = sem("s_rk")
        s_rec = sem("s_rec")
        s_row = sem("s_row")
        s_scat = sem("s_scat")
        s_dv = sem("s_dv")
        s_first = sem("s_first")
        s_pq = sem("s_pq")

        xr = x.rearrange("b (t p) d -> (b t) p d", p=P)
        outr = x1_out.rearrange("b (t p) d -> (b t) p d", p=P)
        x2r = x2_rows[0:T, :].rearrange("(t p) d -> t p d", p=P)
        ctxr = ctx_in.rearrange("b (t p) c -> b p t c", p=P)
        block = st.enter_context(nc.Block())

        @block.sync
        def _(sp):
            def load_x(tile, u):
                sp.dma_start(xin[:, u, :, :], xr[bass.ds(tile, UNIT)].rearrange("t p d -> p t d")
                             ).then_inc(s_xin[u], 16)

            def load_ctx(b):
                sp.dma_start(ctxt[:, :, :], ctxr[bass.ds(b, 1)].rearrange("b p t c -> p (b t) c")
                             ).then_inc(s_ctx, 16)

            sp.dma_start(wk_in[:, :, :], W_k.rearrange("(a p) c -> p a c", p=P)).then_inc(s_wk, 16)
            with nc.allow_non_contiguous_dma(reason="256 elements"):
                sp.dma_start(bk_col[:, :], b_k.rearrange("(a p) -> p a", p=P)).then_inc(s_wk, 16)
            load_ctx(0)
            load_x(0, 0)
            sp.dma_start(gam[:, :], gamma.partition_broadcast(P)).then_inc(s_const, 16)
            sp.dma_start(bet[:, :], beta.partition_broadcast(P)).then_inc(s_const, 16)
            sp.dma_start(gw[:, :, :], gate_w.rearrange("(k p) e -> p k e", p=P)).then_inc(s_gw, 16)
            load_x(UNIT, 1)

            def store(b, what, t, last):
                if what == "x1":
                    sp.wait_ge(s_x1, b * BT + t + 1)
                    sp.dma_start(outr[bass.ds(b * BT + t, 1)].rearrange("t p d -> (t p) d"),
                                 x1[:, t % 2, :]).then_inc(s_st[t % 2], 16)
                    if t % UNIT == UNIT - 1 and not last:
                        load_x(b * BT + t - (UNIT - 1) + BT, t // UNIT)
                elif what == "x2":
                    sp.wait_ge(s_x2, b * BT + t + 1)
                    sp.dma_start(x2r[bass.ds(b * BT + t, 1)].rearrange("t p d -> (t p) d"),
                                 x2[:, t % 2, :]).then_inc(s_st[t % 2], 16)

            def body(b, last):
                if not last:
                    sp.wait_ge(s_ev, b * RING_B + RING_PRE)
                    load_ctx(b + 1)
                for what, t in BODY[last]:
                    store(b, what, t, last)

            for what, t in PROLOGUE:
                store(0, what, t, False)
            with sp.Fori(0, BATCH - 1) as b:
                body(b, False)
            body(BATCH - 1, True)
            sp.wait_ge(s_first, 1)
            first_weights(sp, first)
            for i in range(2):
                sp.wait_ge(s_st[i], BATCH * BT // 2 * 32 + 32)

        @block.gpsimd
        def _(pool):
            step = Chain(pool, s_pool, 0, 14)
            nc.gpsimd.memset(leps[:, :], LN_EPS).then_inc(s_mask, 1)
            nc.gpsimd.memset(seps[:, :], SIM_EPS / SIM_SCALE ** 2).then_inc(s_mask, 1)
            nc.gpsimd.memset(onesm[:, :], 1.0).then_inc(s_mask, 1)
            nc.gpsimd.memset(zrow[:, :], 0.0).then_inc(s_mask, 1)
            nc.gpsimd.memset(mhalf[:, :], -0.5).then_inc(s_mask, 1)
            nc.gpsimd.memset(both[:, BT, :], 0.0).then_inc(s_mask, 1)
            step(nc.gpsimd.memset(ident[:, :], 1.0))
            step(nc.gpsimd.affine_select(out=ident[:, :], in_=ident[:, :], compare_op=ALU.is_equal, fill=0.0,
                                         base=0, pattern=[[1, P]], channel_multiplier=-1))
            step(nc.gpsimd.memset(before[:, :], 1.0))
            step(nc.gpsimd.affine_select(out=before[:, :], in_=before[:, :], compare_op=ALU.is_gt, fill=0.0,
                                         base=0, pattern=[[1, P]], channel_multiplier=-1))
            step(nc.gpsimd.iota(pref[:, :], [[-1, E]], base=E, channel_multiplier=0))
            step(nc.gpsimd.tensor_copy(preff[:, :], pref[:, :]))
            step(nc.gpsimd.tensor_scalar(eidf[:, :], preff[:, :], -1.0, float(E), ALU.mult, ALU.add))
            step(nc.gpsimd.tensor_scalar(ebase[:, :], eidf[:, :], float(LIST), None, ALU.mult))
            step(nc.gpsimd.tensor_copy(lbase[:, :], ebase[:, :]))
            step(nc.gpsimd.iota(seqs[:, :], [[0, BT]], base=SEQ, channel_multiplier=0))
            step(nc.gpsimd.iota(sidx[:, :, :], [[1, META], [0, E]], base=0, channel_multiplier=0))
            step(nc.gpsimd.iota(empty[:, :, 0:1], [[0, TAB // P], [0, 1]], base=NOROW, channel_multiplier=0))
            step(nc.gpsimd.iota(empty[:, :, 1:2], [[0, TAB // P], [0, 1]], base=0, channel_multiplier=0))
            nc.gpsimd.iota(rowid[:, :], [[P, BT]], base=0, channel_multiplier=1).then_inc(s_row, 1)
            nc.gpsimd.iota(rec[:, :, :, 0], [[0, 2], [0, BT]], base=NOROW, channel_multiplier=0).then_inc(s_mask, 1)
            nc.gpsimd.iota(rec[:, :, :, 1], [[0, 2], [0, BT]], base=0, channel_multiplier=0).then_inc(s_mask, 1)
            step(nc.gpsimd.iota(posi[:, :, :], [[BT * P, 2], [P, BT]], base=PADROW, channel_multiplier=1))
            step.close()
            pool.dma_start(table.rearrange("(p n) c -> p (n c)", p=P),
                           empty[:, :, :].rearrange("p n c -> p (n c)")).then_inc(s_init, 16)
            pool.wait_ge(s_mask, 8)
            pool.dma_start(x2_rows[T:T + 1, :], zrow[:, :]).then_inc(s_init, 16)

            def rstd(step, b, what, t):
                i = t % 2
                if what == "xstats":
                    pool.wait_ge(s_mva, b * UNITS + t // UNIT + 1)
                    step(nc.gpsimd.tensor_tensor(ve[:, 0:UNIT], mv_a[:, :, 1], leps[:, :], ALU.add))
                    nc.gpsimd.tensor_tensor(rs_a[:, :], ve[:, 0:UNIT], mhalf[:, :], ALU.pow).then_inc(s_rsa, 1)
                elif what == "stats":
                    pool.wait_ge(s_mvs, b * BT + t + 1)
                    step(nc.gpsimd.tensor_tensor(ve[:, 4 + i:5 + i], mv_s[:, i, 1:2], seps[:, :], ALU.add))
                    nc.gpsimd.tensor_tensor(rs_s[:, i:i + 1], ve[:, 4 + i:5 + i], mhalf[:, 0:1], ALU.pow
                                            ).then_inc(s_rss, 1)
                elif what == "x1":
                    pool.wait_ge(s_mvb, b * BT + t + 1)
                    step(nc.gpsimd.tensor_tensor(ve[:, 8 + i:9 + i], mv_b[:, i, 1:2], leps[:, 0:1], ALU.add))
                    nc.gpsimd.tensor_tensor(rs_b[:, i:i + 1], ve[:, 8 + i:9 + i], mhalf[:, 0:1], ALU.pow
                                            ).then_inc(s_rsb, 1)

            def scatter(i):
                c, t = i // BT, i % BT
                pool.indirect_dma_start(
                    out=table, out_offset=bass.IndirectOffsetOnAxis(ap=posi[:, c, t:t + 1], axis=0),
                    in_=rec[:, c, t, :], in_offset=None).then_inc(s_scat, 16)

            def body(b, last):
                step = Chain(pool, s_pq, b * POOL_STEPS + POOL_PRE, POOL_STEPS - (POOL_PRE if last else 0))
                sets = 0
                for what, t in BODY[last]:
                    rstd(step, b, what, t)
                    if what in ("x1", "x2"):
                        for _ in range(2 if last else 1):
                            if sets < 2 * BT:
                                scatter(sets)
                                sets += 1
                assert sets == 2 * BT
                step.close()
                pool.wait_ge(s_rec, b + 1)
                nc.gpsimd.tensor_tensor(rowid[:, :], rowid[:, :], seqs[:, :], ALU.add).then_inc(s_row, 1)

            step = Chain(pool, s_pq, 0, POOL_PRE)
            for what, t in PROLOGUE:
                rstd(step, 0, what, t)
            step.close()
            pool.wait_ge(s_init, 32)
            with pool.Fori(0, BATCH - 1) as b:
                body(b, False)
            body(BATCH - 1, True)
            for i in range(2 * BT):
                scatter(i)
            pool.wait_ge(s_scat, (BATCH + 1) * 2 * BT * 16)

        @block.tensor
        def _(pe):
            def free(n, g0):
                if not (isinstance(g0, int) and g0 + n < RING):
                    pe.wait_ge(s_ev, g0 + n - (RING - 1))

            def turn(n, g0, source):
                free(n, g0)
                for j, a in enumerate(source):
                    mm = pe.transpose(ring[:, n % RING, j * P:(j + 1) * P], a, ident[:, :])
                mm.then_inc(s_ring, 1)

            def stage(b, g0, n, what, t, last):
                if what == "ctxT":
                    pe.wait_ge(s_ctx, 16 * b + 16 * (t // BT) + 16)
                    for c in range(2):
                        for jh in range(2):
                            turn(n, g0, [ctxt[:, jh * 4 + j, c * P:(c + 1) * P] for j in range(4)])
                            n += 1
                elif what == "kvT":
                    pe.wait_ge(s_ev, g0 + n)
                    for dc in range(2):
                        for jh in range(2):
                            free(n, g0)
                            for c in range(2):
                                mm = pe.matmul(ring[:, n % RING, :], wkT[:, c, dc * P:(dc + 1) * P],
                                               ctxT[:, c, jh * BANK:(jh + 1) * BANK], start=(c == 0), stop=(c == 1))
                            mm.then_inc(s_ring, 1)
                            n += 1
                elif what == "kv":
                    pe.wait_ge(s_ev, g0 + filled_after(last, "kvT", t))
                    for q in range(BT // 2):
                        turn(n, g0, [kvT[:, dc, (2 * q + h) * P:(2 * q + h + 1) * P] for h in range(2)
                                     for dc in range(2)])
                        n += 1
                elif what == "turn1":
                    pe.wait_ge(s_pn, b * BT + t + 1)
                    for h in range(2):
                        turn(n, g0, [pn[:, t % 2, k * P:(k + 1) * P] for k in range(4 * h, 4 * h + 4)])
                        n += 1
                elif what in ("outA", "outB"):
                    dc = int(what == "outB")
                    if dc == 0:
                        pe.wait_ge(s_ev, g0 + n)
                    free(n, g0)
                    for k in range(KT):
                        mm = pe.matmul(ring[:, n % RING, :], kv[:, k, dc * P:(dc + 1) * P], pT[:, k, :],
                                       start=(k == 0), stop=(k == KT - 1))
                    mm.then_inc(s_ring, 1)
                    n += 1
                elif what == "sim":
                    if t % UNIT == 0:
                        pe.wait_ge(s_ev, g0 + filled_after(last, "outB", t))
                    if not (isinstance(b, int) and b * BT + t < 2):
                        pe.wait_ge(s_z1, b * BT + t - 1)
                    for h in range(2):
                        for dc in range(2):
                            mm = pe.matmul(simp[:, t % 2, h * BANK:(h + 1) * BANK],
                                           oT[:, dc, (t % UNIT) * P:(t % UNIT + 1) * P],
                                           kvT[:, dc, h * BANK:(h + 1) * BANK], start=(dc == 0), stop=(dc == 1))
                    mm.then_inc(s_sim, 1)
                elif what == "turn2":
                    pe.wait_ge(s_x2, b * BT + t + 1)
                    for h in range(2):
                        turn(n, g0, [x2[:, t % 2, k * P:(k + 1) * P] for k in range(4 * h, 4 * h + 4)])
                        n += 1
                elif what == "logits":
                    pe.wait_ge(s_ev, g0 + filled_after(last, "turn2", t))
                    for k in range(KT):
                        mm = pe.matmul(lgp[:, t, :], x2T[:, t % 2, k, :], gw[:, k, :], start=(k == 0),
                                       stop=(k == KT - 1))
                    mm.then_inc(s_lg, 1)
                elif what == "ranks":
                    pe.wait_ge(s_both, b + 1)
                    pe.matmul(rkp[:, :, :], before[:, :], both[:, :, :], start=True, stop=False)
                    for q in range(BT):
                        mm = pe.matmul(rkp[:, q + 1:BT + 1, :], onesm[:, :],
                                       both[:, q:q + 1, :].to_broadcast([P, BT - q, E]), start=False,
                                       stop=(q == BT - 1))
                    mm.then_inc(s_rk, 1)
                return n

            def body(b, last):
                n = 0
                for what, t in BODY[last]:
                    n = stage(b, b * RING_B + RING_PRE, n, what, t, last)

            pe.wait_ge(s_pool, 2)
            pe.wait_ge(s_mask, 8)
            pe.wait_ge(s_wk, 32)
            for dc in range(2):
                for c in range(2):
                    mm = pe.transpose(ring[:, dc, c * P:(c + 1) * P], wk_in[:, dc, c * P:(c + 1) * P], ident[:, :])
                mm.then_inc(s_ring, 1)
            n = 2
            for what, t in PROLOGUE:
                n = stage(0, 0, n, what, t, None)
            pe.wait_ge(s_gw, 16)
            with pe.Fori(0, BATCH - 1) as b:
                body(b, False)
            body(BATCH - 1, True)

        @block.scalar
        def _(act):
            act.wait_ge(s_wk, 32)

            def put(g0, n, out, in_):
                act.wait_ge(s_ring, g0 + n + 1)
                nc.scalar.activation(out, in_, ACT.Copy).then_inc(s_ev, 1)
                return n + 1

            def stage(b, g0, n, what, t):
                if what == "ctxT":
                    for c in range(2):
                        for jh in range(2):
                            n = put(g0, n, ctxT[:, c, jh * BANK:(jh + 1) * BANK], ring[:, n % RING, :])
                elif what == "kvT":
                    for dc in range(2):
                        for jh in range(2):
                            act.wait_ge(s_ring, g0 + n + 1)
                            nc.scalar.activation(kvT[:, dc, jh * BANK:(jh + 1) * BANK], ring[:, n % RING, :],
                                                 ACT.Identity, bias=bk_col[:, dc:dc + 1]).then_inc(s_ev, 1)
                            n += 1
                elif what == "kv":
                    for q in range(BT // 2):
                        n = put(g0, n, kv[:, 2 * q:2 * q + 2, :],
                                ring[:, n % RING, :].rearrange("p (h c) -> p h c", h=2))
                elif what == "turn1":
                    r = t % UNIT * P
                    for h in range(2):
                        n = put(g0, n, pT[:, 4 * h:4 * h + 4, r:r + P],
                                ring[:, n % RING, :].rearrange("p (k i) -> p k i", k=4))
                elif what == "choices":
                    act.wait_ge(s_lgr, b + 1)
                    nc.scalar.activation(pr[:, :, :], lg[:, :, :], ACT.Exp).then_inc(s_pe, 1)
                elif what in ("outA", "outB"):
                    n = put(g0, n, oT[:, int(what == "outB"), :], ring[:, n % RING, :])
                elif what == "exp":
                    act.wait_ge(s_nmx, b * BT + t + 1)
                    nc.scalar.activation(z[:, t % 2, :], z[:, t % 2, :], ACT.Exp, bias=nmx[:, t % 2:t % 2 + 1],
                                         accum_out=esum[:, t % 2:t % 2 + 1]).then_inc(s_exp, 1)
                elif what == "turn2":
                    for h in range(2):
                        n = put(g0, n, x2T[:, t % 2, 4 * h:4 * h + 4, :],
                                ring[:, n % RING, :].rearrange("p (k i) -> p k i", k=4))
                return n

            def body(b, last):
                n = 0
                for what, t in BODY[last]:
                    n = stage(b, b * RING_B + RING_PRE, n, what, t)

            n = 0
            for dc in range(2):
                n = put(0, n, wkT[:, :, dc * P:(dc + 1) * P], ring[:, dc, 0:2 * P].rearrange("p (c j) -> p c j", c=2))
            for what, t in PROLOGUE:
                n = stage(0, 0, n, what, t)
            assert n == RING_PRE
            with act.Fori(0, BATCH - 1) as b:
                body(b, False)
            body(BATCH - 1, True)

        @block.vector
        def _(dve):
            V = nc.vector
            for i in range(2):
                V.memset(x1[:, i, 0:1], 0.0).then_inc(s_st[i], 32)

            def stage(step, b, what, t, turned):
                i = t % 2
                if what == "xstats":
                    u = t // UNIT % UNITS
                    dve.wait_ge(s_xin[u], b * 16 + 16 * (t // BT) + 16)
                    for r in range(UNIT):
                        V.bn_stats(st_a[:, r, 0, :], xin[:, u, r, 0:BANK])
                        V.bn_stats(st_a[:, r, 1, :], xin[:, u, r, BANK:D])
                    dve.drain()
                    for r in range(UNIT):
                        done = V.bn_aggr(mv_a[:, r, :], st_a[:, r, :, :].rearrange("p a s -> p (a s)"))
                    done.then_inc(s_mva, 1)
                elif what == "norm":
                    r, u = t % UNIT, t // UNIT % UNITS
                    if r == 0:
                        dve.wait_ge(s_mva, b * UNITS + t // UNIT + 1)
                        dve.wait_ge(s_rsa, b * UNITS + t // UNIT + 1)
                    if r >= 2:
                        dve.wait_ge(s_ring, turned)
                    V.tensor_scalar(pn[:, i, :], xin[:, u, r, :], mv_a[:, r, 0:1], rs_a[:, r:r + 1],
                                    ALU.subtract, ALU.mult).then_inc(s_pn, 1)
                elif what == "stats":
                    dve.wait_ge(s_sim, b * BT + t + 1)
                    V.bn_stats(st_s[:, i, 0, :], simp[:, i, 0:BANK])
                    V.bn_stats(st_s[:, i, 1, :], simp[:, i, BANK:D])
                    dve.drain()
                    V.bn_aggr(mv_s[:, i, :], st_s[:, i, :, :].rearrange("p a s -> p (a s)")).then_inc(s_mvs, 1)
                elif what == "scores":
                    dve.wait_ge(s_mvs, b * BT + t + 1)
                    zt = z[:, i, :]
                    V.scalar_tensor_tensor(out=zt, in0=simp[:, i, :], scalar=mv_s[:, i, 0:1], in1=gam[:, :],
                                           op0=ALU.subtract, op1=ALU.mult).then_inc(s_z1, 1)
                    dve.wait_ge(s_rss, b * BT + t + 1)
                    dve.wait_ge(s_z1, b * BT + t + 1)
                    step(V.scalar_tensor_tensor(out=zt, in0=zt, scalar=rs_s[:, i:i + 1], in1=bet[:, :],
                                                op0=ALU.mult, op1=ALU.add))
                    V.tensor_reduce(nmx[:, i:i + 1], zt, AX.X, ALU.max, negate=True).then_inc(s_nmx, 1)
                elif what == "x1":
                    dve.wait_ge(s_exp, b * BT + t + 1)
                    step(V.reciprocal(rsum[:, i:i + 1], esum[:, i:i + 1]))
                    dve.wait_ge(s_st[i], b * (BT // 2 * 32) + 32 * (t // 2) + 32)
                    V.scalar_tensor_tensor(out=x1[:, i, :], in0=z[:, i, :], scalar=rsum[:, i:i + 1],
                                           in1=xin[:, t // UNIT, t % UNIT, :], op0=ALU.mult, op1=ALU.add
                                           ).then_inc(s_x1, 1)
                    dve.wait_ge(s_x1, b * BT + t + 1)
                    V.bn_stats(st_b[:, i, 0, :], x1[:, i, 0:BANK])
                    V.bn_stats(st_b[:, i, 1, :], x1[:, i, BANK:D])
                    dve.drain()
                    V.bn_aggr(mv_b[:, i, :], st_b[:, i, :, :].rearrange("p a s -> p (a s)")).then_inc(s_mvb, 1)
                elif what == "x2":
                    dve.wait_ge(s_mvb, b * BT + t + 1)
                    dve.wait_ge(s_rsb, b * BT + t + 1)
                    if t >= 2:
                        dve.wait_ge(s_ring, turned)
                    V.tensor_scalar(x2[:, i, :], x1[:, i, :], mv_b[:, i, 0:1], rs_b[:, i:i + 1],
                                    ALU.subtract, ALU.mult).then_inc(s_x2, 1)
                elif what == "choices":
                    choices(step, b)
                elif what == "places":
                    places(step, b)

            def choices(step, b):
                def wide(a):
                    return a.unsqueeze(2).to_broadcast([P, BT, E])

                def pref_b():
                    return preff[:, :].unsqueeze(1).to_broadcast([P, BT, E])

                dve.wait_ge(s_lg, b * BT + BT)
                step(V.tensor_reduce(m1[:, :], lgp, AX.X, ALU.max))
                V.tensor_tensor(lg[:, :, :], lgp, wide(m1[:, :]), ALU.subtract).then_inc(s_lgr, 1)
                dve.wait_ge(s_pe, b + 1)
                step(V.tensor_reduce(msum[:, :], pr[:, :, :], AX.X, ALU.add))
                step(V.reciprocal(m2[:, :], msum[:, :]))
                step(V.tensor_tensor(pr[:, :, :], pr[:, :, :], wide(m2[:, :]), ALU.mult))

                def choose(top, onehot):
                    step(V.tensor_reduce(top, pr[:, :, :], AX.X, ALU.max))
                    step(V.tensor_tensor(t0[:, :, :], pr[:, :, :], wide(top), ALU.is_equal))
                    step(V.tensor_tensor(t0[:, :, :], t0[:, :, :], pref_b(), ALU.mult))
                    step(V.tensor_reduce(mk[:, :], t0[:, :, :], AX.X, ALU.max))
                    step(V.tensor_tensor(onehot, t0[:, :, :], wide(mk[:, :]), ALU.is_equal))

                choose(m1[:, :], oh1[:, :, :])
                step(V.scalar_tensor_tensor(out=pr[:, :, :], in0=oh1[:, :, :], scalar=-2.0, in1=pr[:, :, :],
                                            op0=ALU.mult, op1=ALU.add))
                choose(m2[:, :], oh2[:, :, :])
                V.tensor_tensor(both[:, 0:BT, :], oh1[:, :, :], oh2[:, :, :], ALU.add).then_inc(s_both, 1)
                step(V.tensor_tensor(msum[:, :], m1[:, :], m2[:, :], ALU.add))
                step(V.reciprocal(mk[:, :], msum[:, :]))
                dve.wait_ge(s_scat, b * (2 * BT * 16) + 2 * BT * 16)
                dve.wait_ge(s_row, b + 1)
                for c, top in enumerate((m1, m2)):
                    V.tensor_tensor(rec[:, c, :, 1].bitcast(F32), top[:, :], mk[:, :], ALU.mult)
                    step(V.tensor_copy(rec[:, c, :, 0], rowid[:, :]))

            def places(step, b):
                dve.wait_ge(s_rk, b + 1)
                step(V.tensor_tensor(t0[:, :, :], rkp[:, 0:BT, :],
                                     lbase[:, :].unsqueeze(1).to_broadcast([P, BT, E]), ALU.add))
                for c, oh in enumerate((oh1, oh2)):
                    step(V.tensor_tensor(oh[:, :, :], oh[:, :, :], t0[:, :, :], ALU.mult))
                    step(V.tensor_reduce(posf[:, c, :], oh[:, :, :], AX.X, ALU.add))
                step(V.tensor_tensor(lbase[:, :], lbase[:, :], rkp[:, BT, :], ALU.add))
                V.tensor_copy(posi[:, :, :], posf[:, :, :]).then_inc(s_rec, 1)

            step = Chain(dve, s_dv, 0, DV_PRE)
            for what, t in PROLOGUE:
                if (what, t) == ("stats", 1):
                    dve.wait_ge(s_pool, 14)
                    dve.wait_ge(s_const, 32)
                stage(step, 0, what, t, 0 if t % UNIT < 2 else filled_after(None, "turn1", t - 2))
            step.close()

            def body(b, last):
                step = Chain(dve, s_dv, b * DV_STEPS + DV_PRE, DV_STEPS - (DV_PRE if last else 0))
                for what, t in BODY[last]:
                    turned = 0
                    if what == "norm" and t % UNIT >= 2:
                        turned = filled_after(last, "turn1", t - 2)
                    elif what == "x2" and t >= 2:
                        turned = filled_after(last, "turn2", t - 2)
                    stage(step, b, what, t, b * RING_B + RING_PRE + turned)
                step.close()

            with dve.Fori(0, BATCH - 1) as b:
                body(b, False)
            body(BATCH - 1, True)

            step = Chain(dve, s_dv, BATCH * DV_STEPS, META_STEPS)
            cnt, has, blk, nsl, two, end, beg = (c8[:, i, :] for i in range(7))
            tmp, tm2 = c8[:, 8, :], c8[:, 9, :]
            step(V.tensor_tensor(cnt, lbase[:, :], ebase[:, :], ALU.subtract))
            step(V.tensor_scalar(has, cnt, 1.0, None, ALU.min))
            step(V.tensor_scalar(i8[:, 0, :], cnt, float(P - 1), None, ALU.add))
            step(V.tensor_scalar(i8[:, 1, :], i8[:, 0, :], 7, None, ALU.logical_shift_right))
            step(V.tensor_copy(tmp, i8[:, 1, :]))
            step(V.tensor_scalar(tmp, tmp, 2.0, None, ALU.max))
            step(V.tensor_tensor(blk, tmp, has, ALU.mult))
            step(V.tensor_scalar(i8[:, 0, :], blk, 2.0, 86.0, ALU.add, ALU.mult))
            step(V.tensor_scalar(i8[:, 1, :], i8[:, 0, :], 8, None, ALU.logical_shift_right))
            step(V.tensor_copy(nsl, i8[:, 1, :]))
            step(V.scalar_tensor_tensor(out=two, in0=nsl, scalar=3.0, in1=blk, op0=ALU.mult, op1=ALU.subtract))
            step(V.tensor_copy(tm2[:, 0:1], nsl[:, 0:1]))
            step(V.tensor_tensor(tm2[:, 1:E], nsl[:, 1:E], nsl[:, 0:E - 1], ALU.add))
            step(V.tensor_copy(tmp[:, 0:2], tm2[:, 0:2]))
            step(V.tensor_tensor(tmp[:, 2:E], tm2[:, 2:E], tm2[:, 0:E - 2], ALU.add))
            step(V.tensor_copy(end[:, 0:4], tmp[:, 0:4]))
            step(V.tensor_tensor(end[:, 4:E], tmp[:, 4:E], tmp[:, 0:E - 4], ALU.add))
            step(V.tensor_scalar(tmp, end, 0.0, None, ALU.is_equal))
            step(V.tensor_reduce(tm2[:, 0:1], tmp, AX.X, ALU.add))
            V.tensor_copy(first[:, :], tm2[0:1, 0:1]).then_inc(s_first, 1)
            step(V.tensor_tensor(beg, end, nsl, ALU.subtract))

            def by_slot(a):
                return a[0:1, :].unsqueeze(1).to_broadcast([1, META, E])

            s_i, mine, i_in, start, t_a, t_b = (sl[:, i, :, :] for i in range(6))
            step(V.tensor_copy(s_i, sidx[:, :, :]))
            step(V.tensor_tensor(t_a, s_i, by_slot(beg), ALU.is_ge))
            step(V.tensor_tensor(t_b, s_i, by_slot(end), ALU.is_lt))
            step(V.tensor_tensor(mine, t_a, t_b, ALU.mult))
            step(V.tensor_tensor(i_in, s_i, by_slot(beg), ALU.subtract))
            step(V.tensor_tensor(t_a, i_in, by_slot(two), ALU.min))
            step(V.scalar_tensor_tensor(out=start, in0=i_in, scalar=float(SB), in1=t_a, op0=ALU.mult,
                                        op1=ALU.subtract))
            step(V.scalar_tensor_tensor(out=t_a, in0=start, scalar=float(P), in1=by_slot(ebase[:, :]), op0=ALU.mult,
                                        op1=ALU.add))
            step(V.tensor_tensor(t_a, t_a, mine, ALU.mult))
            step(V.tensor_reduce(metaf[:, 1, :], t_a, AX.X, ALU.add))
            step(V.scalar_tensor_tensor(out=t_a, in0=start, scalar=float(-P), in1=by_slot(cnt), op0=ALU.mult,
                                        op1=ALU.add))
            step(V.tensor_scalar(t_a, t_a, float(2 * P), None, ALU.max))
            step(V.tensor_tensor(t_b, i_in, by_slot(two), ALU.is_lt))
            step(V.tensor_scalar(t_b, t_b, float(-P), float(SB * P), ALU.mult, ALU.add))
            step(V.tensor_tensor(t_a, t_a, t_b, ALU.min))
            step(V.tensor_tensor(t_a, t_a, mine, ALU.mult))
            step(V.tensor_reduce(metaf[:, 0, :], t_a, AX.X, ALU.add))
            step(V.tensor_scalar(im[:, 0, :], metaf[:, 0, :], float(GROUP - 1), None, ALU.add))
            step(V.tensor_scalar(im[:, 1, :], im[:, 0, :], 5, None, ALU.logical_shift_right))
            step(V.tensor_copy(metaf[:, 3, :], im[:, 1, :]))
            step(V.tensor_tensor(t_a, mine, by_slot(eidf[:, :]), ALU.mult))
            step(V.tensor_reduce(metaf[:, 0, :], t_a, AX.X, ALU.add))
            is3, pl = sl[:, 6, :, 0], sl[:, 7, :, 0]
            step(V.tensor_scalar(is3, metaf[:, 3, :], float(2 * P // GROUP), None, ALU.is_gt))
            step(V.tensor_scalar(pl, metaf[:, 1, :], float(2 * P - PADROW), None, ALU.add))
            step(V.tensor_tensor(pl, pl, is3, ALU.mult))
            step(V.tensor_scalar(metaf[:, 2, :], pl, float(PADROW), None, ALU.add))
            step(V.tensor_copy(meta[:, :, :], metaf[:, :, :]))
            step.close()


UNIT_STEPS = [("sim", 0, 2), ("scores", 0, 0), ("exp", 0, 0), ("choices", 0, 0), ("ranks", 0, 0), ("scores", 0, 1),
              ("places", 0, 0), ("x1", 0, 0), ("ctxT", 1, 0), ("stats", 0, 2), ("x2", 0, 0), ("exp", 0, 1),
              ("sim", 0, 3), ("kvT", 1, 0), ("turn2", 0, 0), ("xstats", 1, 0), ("x1", 0, 1), ("norm", 1, 0),
              ("kv", 1, 0), ("norm", 1, 1), ("logits", 0, 0), ("turn1", 1, 0), ("norm", 1, 2), ("turn1", 1, 1),
              ("turn1", 1, 2), ("norm", 1, 3), ("turn1", 1, 3), ("scores", 0, 2), ("stats", 0, 3), ("x2", 0, 1),
              ("exp", 0, 2), ("outA", 1, 0), ("turn2", 0, 1), ("outB", 1, 0), ("scores", 0, 3), ("x1", 0, 2),
              ("logits", 0, 1), ("exp", 0, 3), ("sim", 1, 0), ("x1", 0, 3), ("sim", 1, 1), ("x2", 0, 2),
              ("stats", 1, 0), ("x2", 0, 3), ("stats", 1, 1), ("turn2", 0, 2), ("turn2", 0, 3), ("logits", 0, 2),
              ("logits", 0, 3)]


def unit_order(u, last):
    next_batch = u == UNITS - 1
    return [(what, (u + later) * UNIT + r) for what, later, r in UNIT_STEPS
            if not (what in CONTEXT and not next_batch) and not (later and next_batch and last)
            and what not in ROUTING]


def ring_after(steps):
    size = {"ctxT": 4, "kvT": 4, "kv": 4, "turn1": 2, "outA": 1, "outB": 1, "turn2": 2}
    n, after = 0, {}
    for step in steps:
        n += size.get(step[0], 0)
        after[step] = n
    return n, after


def body_order(last):
    steps = [step for u in range(UNITS) for step in unit_order(u, last)][len(HEAD):]
    if last:
        return steps + [(what, 0) for what in ROUTING]
    return steps + [(what, t if what in ROUTING else t + BT) for what, t in HEAD_ROUTED]


def filled_after(last, what, t):
    if last is None:
        return AFTER_PRE[what, t]
    if (what, t) in AFTER[last]:
        return AFTER[last][what, t]
    return AFTER[False][what, t + BT] - RING_B


ROUTING = ("choices", "ranks", "places")
CONTEXT = ("ctxT", "kvT", "kv")
HEAD_ROUTED = [(what, 0 if what in ROUTING else later * UNIT + r)
               for what, later, r in UNIT_STEPS[:UNIT_STEPS.index(("places", 0, 0)) + 1] if what not in CONTEXT]
HEAD = [step for step in HEAD_ROUTED if step[0] not in ROUTING]
PROLOGUE = [("ctxT", 0), ("kvT", 0), ("xstats", 0), ("norm", 0), ("norm", 1), ("turn1", 0), ("turn1", 1), ("kv", 0),
            ("norm", 2), ("norm", 3), ("turn1", 2), ("turn1", 3), ("outA", 0), ("outB", 0), ("sim", 0), ("stats", 0),
            ("sim", 1), ("stats", 1)] + HEAD
BODY = {last: body_order(last) for last in (False, True)}
AFTER = {last: ring_after(BODY[last])[1] for last in (False, True)}
RING_PRE, AFTER_PRE = ring_after([("turn2", -1)] + PROLOGUE)
RING_B = ring_after(BODY[False])[0]
POOL_PRE = sum(what in ("xstats", "stats", "x1") for what, t in PROLOGUE)
POOL_STEPS = UNITS + 2 * BT
DV_PRE = sum(what in ("scores", "x1") for what, t in PROLOGUE)
DV_STEPS = 2 * BT + 1 + 3 + 5 + 1 + 5 + 2 + 2 + 1 + 4 + 1


def experts(nc, w1, w3, w2, out, x2_rows, table, meta, raw13_0, raw2_0, s_raw13_0, s_raw2_0):
    with ExitStack() as st:
        def sb(name, shape, dt=F32):
            return st.enter_context(nc.sbuf_tensor(name, shape, dt))

        def sem(name):
            return st.enter_context(nc.semaphore(name))

        raw13 = [raw13_0, sb("raw13_1", [P, 2, KT, 2 * P])]
        raw2 = [raw2_0, sb("raw2_1", [P, 2, D])]
        hi13 = [sb(f"hi13_{i}", [P, 2, KT, P], F32R) for i in range(2)]
        lo13 = [sb(f"lo13_{i}", [P, 2, KT, P], F32R) for i in range(2)]
        hi2 = [sb(f"hi2_{i}", [P, D], F32R) for i in range(2)]
        lo2 = [sb(f"lo2_{i}", [P, D], F32R) for i in range(2)]
        xg = sb("xg", [P, SB, D])
        xhi = sb("xhi", [P, KT, SB * P], F32R)
        xlo = sb("xlo", [P, KT, SB * P], F32R)
        sil = sb("sil", [P, SB * P])
        hid = sb("hid", [P, SB * P])
        hhi = [sb(f"hhi_{i}", [P, SB * P], F32R) for i in range(2)]
        hlo = [sb(f"hlo_{i}", [P, SB * P], F32R) for i in range(2)]
        y = sb("y", [P, SB, D])
        id_g = sb("id_g", [P, SB, 2], I32)
        id_s = sb("id_s", [P, SB, 2], I32)
        ident = sb("ident2", [P, P])
        ticks = sb("ticks", [P, 3])
        free_at_start = sb("free_at_start", [P, 8])

        p1 = st.enter_context(nc.psum_tensor("p1", [P, BANK], F32))
        p3 = st.enter_context(nc.psum_tensor("p3", [P, BANK], F32))
        acc = st.enter_context(nc.psum_tensor("acc", [P, SB, D], F32))

        s_raw13 = [s_raw13_0, sem("s_raw13_1")]
        s_raw2 = [s_raw2_0, sem("s_raw2_1")]
        s_hi13 = sem("s_hi13")
        s_lo13 = sem("s_lo13")
        s_hi2 = sem("s_hi2")
        s_lo2 = sem("s_lo2")
        s_h1 = sem("s_h1")
        s_h3 = sem("s_h3")
        s_sil = sem("s_sil")
        s_hid = sem("s_hid")
        s_hhi = sem("s_hhi")
        s_hlo = sem("s_hlo")
        s_out = sem("s_out")
        s_t = sem("s_t")
        s_thi = sem("s_thi")
        s_tlo = sem("s_tlo")
        s_ya = sem("s_ya")
        s_yd = sem("s_yd")
        s_idg = sem("s_idg")
        s_ids = sem("s_ids")
        s_xg = sem("s_xg")
        s_sc = sem("s_sc")
        s_added = sem("s_added")
        s_id = sem("s_id")
        s_tick = sem("s_tick")

        out_rows = out.rearrange("b s d -> (b s) d")
        w1v = w1.rearrange("e (k p) m -> e p k m", p=P)
        w3v = w3.rearrange("e (k p) m -> e p k m", p=P)
        w2v = w2.rearrange("e (m p) d -> e p m d", p=P)
        block = st.enter_context(nc.Block())

        def slot_value(eng, row, s, most):
            return eng.value_load(meta[0:1, row, bass.ds(s, 1)], min_val=0, max_val=most)

        @block.sync
        def _(sp):
            def load(e, pair, parity, s):
                sp.wait_ge(s_lo13, s * MT + pair * 2 - 1)
                sp.dma_start(raw13[parity][:, 0], w1v[bass.ds(e, 1), :, :, bass.ds(pair * 2 * P, 2 * P)].rearrange(
                    "e p k m -> (e p) k m")).then_inc(s_raw13[parity], 16)
                sp.dma_start(raw13[parity][:, 1], w3v[bass.ds(e, 1), :, :, bass.ds(pair * 2 * P, 2 * P)].rearrange(
                    "e p k m -> (e p) k m")).then_inc(s_raw13[parity], 16)
                sp.wait_ge(s_lo2, s * MT + pair * 2 - 1)
                sp.dma_start(raw2[parity][:, :, :], w2v[bass.ds(e, 1), :, bass.ds(pair * 2, 2), :].rearrange(
                    "e p m d -> (e p) m d")).then_inc(s_raw2[parity], 16)

            sp.wait_ge(s_xg, SB * 16)
            with sp.Fori(0, SLOTS) as s:
                with sp.If(slot_value(sp, 3, s, WIDTHS[-1]) > 0):
                    e = slot_value(sp, 0, s, E - 1)
                    with sp.Fori(0, MT // 4 - 1) as i:
                        load(e, i * 2 + 1, 1, s)
                        load(e, i * 2 + 2, 0, s)
                    load(e, MT // 2 - 1, 1, s)
                    e = slot_value(sp, 0, s + 1, E - 1)
                    load(e, 0, 0, s + 1)

        @block.scalar
        def _(act):
            def split13(s, fills, par4):
                j, half = par4 // 2, par4 % 2
                act.wait_ge(s_raw13[j], (s * (MT // 4) + fills) * 32)
                nc.scalar.activation(hi13[par4 % 2][:, :, :, :].rearrange("p a k c -> p (a k) c"),
                                     raw13[j][:, :, :, half * P:(half + 1) * P].rearrange("p a k c -> p (a k) c"),
                                     ACT.Copy).then_inc(s_hi13, 1)

            def tile(s, base, q, quad):
                g = s * MT + base
                act.wait_ge(s_h3, g + q + 1)
                split13(s, quad + (1 if q == 3 else 0), (q + 1) % 4)
                act.wait_ge(s_h1, g + q + 1)
                act.wait_ge(s_hid, g + q + 1)
                nc.scalar.activation(sil[:, :], p1[:, 0:SB * P], ACT.Silu).then_inc(s_sil, 1)
                act.wait_ge(s_raw2[q // 2], (s * (MT // 4) + quad) * 16)
                nc.scalar.activation(hi2[q % 2][:, :], raw2[q // 2][:, q % 2, :], ACT.Copy).then_inc(s_hi2, 1)
                act.wait_ge(s_hid, g + q + 2)
                nc.scalar.activation(hhi[q % 2][:, :], hid[:, :], ACT.Copy).then_inc(s_hhi, 1)

            def rows_split(n):
                for q in range(2 * SB):
                    blk, k = q // 2, 4 * (q % 2)
                    act.wait_ge(s_t, n * (2 * SB) + q + 1)
                    nc.scalar.activation(xhi[:, k:k + 4, blk * P:(blk + 1) * P],
                                         (p1, p3)[q % 2][:, :].rearrange("p (k i) -> p k i", k=4),
                                         ACT.Copy).then_inc(s_thi, 1)

            split13(0, 1, 0)
            rows_split(0)
            with act.Fori(0, SLOTS) as s:
                with act.If(slot_value(act, 3, s, WIDTHS[-1]) > 0):
                    with act.Fori(0, MT // 4) as i:
                        for q in range(4):
                            tile(s, i * 4, q, i + 1)
                    rows_split(s + 1)
                    act.wait_ge(s_ids, s * 32 + 32)
                    act.wait_ge(s_out, s + 1)
                    act.wait_ge(s_added, s + 1)
                    for j in range(SB):
                        last = nc.scalar.activation(y[:, j, 0:BANK], acc[:, j, 0:BANK], ACT.Copy,
                                                    scale=id_s[:, j, 1:2].bitcast(F32))
                    last.then_inc(s_ya, 1)

        @block.vector
        def _(dve):
            V = nc.vector

            def split13(s, m, par4):
                j, half = par4 // 2, par4 % 2
                g = s * MT + m
                dve.wait_ge(s_hi13, g + 1)
                V.tensor_tensor(lo13[par4 % 2][:, :, :, :].rearrange("p a k c -> p (a k) c"),
                                raw13[j][:, :, :, half * P:(half + 1) * P].rearrange("p a k c -> p (a k) c"),
                                hi13[par4 % 2][:, :, :, :].rearrange("p a k c -> p (a k) c").bitcast(F32),
                                ALU.subtract).then_inc(s_lo13, 1)

            def tile(s, base, q):
                g = s * MT + base
                split13(s, base + (q + 1), (q + 1) % 4)
                dve.wait_ge(s_h3, g + q + 2)
                dve.wait_ge(s_sil, g + q + 1)
                dve.wait_ge(s_hlo, g + q + 1)
                V.tensor_tensor(hid[:, :], sil[:, :], p3[:, 0:SB * P], ALU.mult).then_inc(s_hid, 1)
                dve.wait_ge(s_hi2, g + q + 1)
                V.tensor_tensor(lo2[q % 2][:, :], raw2[q // 2][:, q % 2, :], hi2[q % 2][:, :].bitcast(F32),
                                ALU.subtract).then_inc(s_lo2, 1)
                dve.wait_ge(s_hhi, g + q + 1)
                V.tensor_tensor(hlo[q % 2][:, :], hid[:, :], hhi[q % 2][:, :].bitcast(F32),
                                ALU.subtract).then_inc(s_hlo, 1)

            def rows_split(n):
                for q in range(2 * SB):
                    blk, k = q // 2, 4 * (q % 2)
                    dve.wait_ge(s_thi, n * (2 * SB) + q + 1)
                    V.tensor_tensor(xlo[:, k:k + 4, blk * P:(blk + 1) * P],
                                    (p1, p3)[q % 2][:, :].rearrange("p (k i) -> p k i", k=4),
                                    xhi[:, k:k + 4, blk * P:(blk + 1) * P].bitcast(F32),
                                    ALU.subtract).then_inc(s_tlo, 1)

            for i, free in enumerate((s_lo13, s_lo2, s_hid, s_hlo, s_yd, s_ya, s_h3)):
                V.memset(free_at_start[:, i:i + 1], 0.0).then_inc(free, 1)
            split13(0, 0, 0)
            rows_split(0)
            with dve.Fori(0, SLOTS) as s:
                with dve.If(slot_value(dve, 3, s, WIDTHS[-1]) > 0):
                    with dve.Fori(0, MT // 4) as i:
                        for q in range(4):
                            tile(s, i * 4, q)
                    rows_split(s + 1)
                    dve.wait_ge(s_ids, s * 32 + 32)
                    dve.wait_ge(s_out, s + 1)
                    dve.wait_ge(s_added, s + 1)
                    for j in range(SB):
                        last = V.tensor_scalar(y[:, j, BANK:D], acc[:, j, BANK:D], id_s[:, j, 1:2].bitcast(F32), None,
                                               ALU.mult)
                    last.then_inc(s_yd, 1)

        @block.tensor
        def _(pe):
            def hidden(s, m, par, n, after_rows):
                g = s * MT + m
                pe.wait_ge(s_lo13, g + 2)
                if after_rows:
                    pe.wait_ge(s_tlo, s * (2 * SB) + 2 * SB)
                else:
                    pe.wait_ge(s_sil, g)
                for a, (bank, done) in enumerate(((p1, s_h1), (p3, s_h3))):
                    if a == 1 and not after_rows:
                        pe.wait_ge(s_hid, g + 1)
                    for k in range(KT):
                        pe.matmul(bank[:, 0:n], hi13[par][:, a, k, :], xhi[:, k, 0:n], start=(k == 0), stop=False)
                        pe.matmul(bank[:, 0:n], hi13[par][:, a, k, :], xlo[:, k, 0:n], start=False, stop=False)
                        mm = pe.matmul(bank[:, 0:n], lo13[par][:, a, k, :], xhi[:, k, 0:n], start=False,
                                       stop=(k == KT - 1))
                    mm.then_inc(done, 1)

            def down_part(par, j, h, first, last):
                o = acc[:, j, h * BANK:(h + 1) * BANK]
                rows, cols = slice(j * P, (j + 1) * P), slice(h * BANK, (h + 1) * BANK)
                pe.matmul(o, hhi[par][:, rows], hi2[par][:, cols], start=first, stop=False)
                pe.matmul(o, hhi[par][:, rows], lo2[par][:, cols], start=False, stop=False)
                return pe.matmul(o, hlo[par][:, rows], hi2[par][:, cols], start=False, stop=last)

            def down_ready(s, m):
                pe.wait_ge(s_hlo, s * MT + m + 2)
                pe.wait_ge(s_lo2, s * MT + m + 2)

            def down(s, m, par, nb, first):
                down_ready(s, m)
                for j in range(nb):
                    for h in range(2):
                        down_part(par, j, h, first, False)

            def turn(n, q, first=False):
                blk, k = q // 2, 4 * (q % 2)
                if q == 0:
                    pe.wait_ge(s_xg, n * (SB * 16) + SB * 16)
                if q >= 2:
                    pe.wait_ge(s_tlo, n * (2 * SB) + q - 1)
                elif not first:
                    pe.wait_ge((s_sil, s_hid)[q], n * MT + q)
                for j in range(4):
                    mm = pe.transpose((p1, p3)[q % 2][:, j * P:(j + 1) * P], xg[:, blk, (k + j) * P:(k + j + 1) * P],
                                      ident[:, :])
                mm.then_inc(s_t, 1)

            def slot(s, n):
                nb = -(-n // P)
                hidden(s, 0, 0, n, True)
                hidden(s, 1, 1, n, False)
                pe.wait_ge(s_ya, s + 1)
                pe.wait_ge(s_yd, s + 1)
                down(s, 0, 0, nb, True)
                with pe.Fori(0, MT // 2 - 2) as i:
                    for j in range(2):
                        hidden(s, i * 2 + (2 + j), j, n, False)
                        down(s, i * 2 + (1 + j), 1 - j, nb, False)
                hidden(s, MT - 2, 0, n, False)
                down(s, MT - 3, 1, nb, False)
                hidden(s, MT - 1, 1, n, False)
                parts = [(par, j, h) for par in range(2) for j in range(nb) for h in range(2)]
                turns = {SB: (2, 3, 5, 6, 8, 9), 2: (2, 3, 4, 5, 6, 7)}[nb]
                for at, (par, j, h) in enumerate(parts):
                    for q in range(2 * SB):
                        if turns[q] == at:
                            turn(s + 1, q)
                    if j == 0 and h == 0:
                        down_ready(s, MT - 2 + par)
                    mm = down_part(par, j, h, False, par == 1)
                mm.then_inc(s_out, 1)

            pe.wait_ge(s_id, 2)
            for h in range(2):
                for c in range(4):
                    pe.transpose(acc[:, SB - 1, h * BANK + c * P:h * BANK + (c + 1) * P], ident[:, :], ident[:, :])
            for q in range(2 * SB):
                turn(0, q, first=True)
            with pe.Fori(0, SLOTS) as s:
                width = slot_value(pe, 3, s, WIDTHS[-1])
                for w in WIDTHS[::-1]:
                    with pe.If(width == w):
                        slot(s, w * GROUP)

        @block.gpsimd
        def _(pool):
            def records(s, to, done):
                place = slot_value(pool, 1, s, E * LIST)
                third = slot_value(pool, 2, s, E * LIST)
                pool.dma_start(to[:, 0:2, :], table[bass.ds(place, 2 * P), :].rearrange("(j p) c -> p j c", p=P)
                               ).then_inc(done, 16)
                pool.dma_start(to[:, 2, :], table[bass.ds(third, P), :]).then_inc(done, 16)

            def tick(n):
                pool.wait_ge(s_tick, n + 1)
                nc.gpsimd.tensor_tensor(ticks[:, 0:1], ticks[:, 0:1], ticks[:, 1:2], ALU.add).then_inc(s_tick, 1)

            def gather(n, ticked):
                records(n, id_g, s_idg)
                pool.wait_ge(s_idg, n * 32 + 32)
                tick(ticked)
                for j in range(SB):
                    pool.indirect_dma_start(out=xg[:, j, :], out_offset=None, in_=x2_rows,
                                            in_offset=bass.IndirectOffsetOnAxis(ap=id_g[:, j, 0:1], axis=0)
                                            ).then_inc(s_xg, 16)

            nc.gpsimd.memset(free_at_start[:, 7:8], 0.0).then_inc(s_added, 1)
            nc.gpsimd.memset(ticks[:, :], 0.0).then_inc(s_tick, 1)
            gather(0, 0)
            nc.gpsimd.memset(ident[:, :], 1.0).then_inc(s_id, 1)
            pool.wait_ge(s_id, 1)
            nc.gpsimd.affine_select(out=ident[:, :], in_=ident[:, :], compare_op=ALU.is_equal, fill=0.0,
                                    base=0, pattern=[[1, P]], channel_multiplier=-1).then_inc(s_id, 1)
            with pool.Fori(0, SLOTS) as s:
                with pool.If(slot_value(pool, 3, s, WIDTHS[-1]) > 0):
                    pool.wait_ge(s_t, s * (2 * SB) + 2 * SB)
                    pool.wait_ge(s_xg, s * (SB * 16) + SB * 16)
                    gather(s + 1, s * 2 + 1)
                    records(s, id_s, s_ids)
                    pool.wait_ge(s_ids, s * 32 + 32)
                    pool.wait_ge(s_ya, s + 2)
                    pool.wait_ge(s_yd, s + 2)
                    tick(s * 2 + 2)
                    for j in range(SB):
                        pool.indirect_dma_start(
                            out=out_rows, out_offset=bass.IndirectOffsetOnAxis(ap=id_s[:, j, 0:1], axis=0),
                            in_=y[:, j, :], in_offset=None, compute_op=ALU.add, bounds_check=T - 1,
                            oob_is_err=False).then_inc(s_sc, 16)
                    pool.wait_ge(s_sc, s * (SB * 16) + SB * 16)
                    pool.wait_ge(s_added, s + 1)
                    pool.wait_ge(s_raw2[0], s * (MT // 4 * 16) + (MT // 4 * 16 + 16))
                    nc.gpsimd.tensor_tensor(ticks[:, 2:3], ticks[:, 2:3], ticks[:, 1:2], ALU.add
                                            ).then_inc(s_added, 1)


def moe_kernel(nc, x, ctx_in, W_k, b_k, gamma, beta, gate_w, w1, w2, w3, out):
    x2_rows = nc.dram_tensor("x2_rows", [T + 1, D], F32, kind="Internal").ap()
    table = nc.dram_tensor("table", [TAB, 2], I32, kind="Internal").ap()
    with ExitStack() as st:
        meta = st.enter_context(nc.sbuf_tensor("meta", [1, 4, META], I32))
        raw13_0 = st.enter_context(nc.sbuf_tensor("raw13_0", [P, 2, KT, 2 * P], F32))
        raw2_0 = st.enter_context(nc.sbuf_tensor("raw2_0", [P, 2, D], F32))
        s_raw13_0 = st.enter_context(nc.semaphore("s_raw13_0"))
        s_raw2_0 = st.enter_context(nc.semaphore("s_raw2_0"))
        attend_and_route(nc, x, ctx_in, W_k, b_k, gamma, beta, gate_w, out, x2_rows, table, meta,
                         lambda sp, first: load_first(sp, first, w1, w3, w2, raw13_0, raw2_0, s_raw13_0, s_raw2_0))
        experts(nc, w1, w3, w2, out, x2_rows, table, meta, raw13_0, raw2_0, s_raw13_0, s_raw2_0)


_INS = ['x', 'ctx_512', 'L0_xattn_W_k', 'L0_xattn_b_k', 'L0_xattn_ln_gamma', 'L0_xattn_ln_beta', 'L0_ffn_gate_w',
        'L0_ffn_w1', 'L0_ffn_w2', 'L0_ffn_w3']


def kernel(**inputs):
    import numpy as _np
    import concourse.bacc as _bacc
    from concourse.bass_utils import run_bass_kernel_spmd as _run

    nc = _bacc.Bacc("TRN2", target_bir_lowering=False, num_devices=1)
    arrays, args = {}, []
    for name in _INS:
        a = _np.ascontiguousarray(inputs[name])
        arrays[f"in_{name}"] = a
        args.append(nc.dram_tensor(f"in_{name}", a.shape, mybir.dt.from_np(a.dtype), kind="ExternalInput").ap())
    args.append(nc.dram_tensor("out_x", (BATCH, SEQ, D), F32, kind="ExternalOutput").ap())
    moe_kernel(nc, *args)
    r = _run(nc, [arrays], core_ids=[0])
    return r.results[0]["out_x"]
```
